# Optimizing a Trainium2 kernel written in Bass

```python
import numpy as np
import jax
import jax.numpy as jnp

def _softmax(x, axis=-1):
    return jax.nn.softmax(x, axis=axis)

def _gelu(x):
    return jax.nn.gelu(x, approximate=True)

def _silu(x):
    return jax.nn.silu(x)

def _sigmoid(x):
    return jax.nn.sigmoid(x)

def _layernorm(x, axis=-1, eps=1e-05):
    m = jnp.mean(x, axis=axis, keepdims=True)
    v = jnp.var(x, axis=axis, keepdims=True)
    return (x - m) / jnp.sqrt(v + eps)

def _scatter_add(tgt, idx, src, axis=0):
    return tgt.at[idx].add(src)

def _segment_sum(src, seg, n):
    return jax.ops.segment_sum(src, seg, n)
kernel_name = 'mk_adaln_d1_jaxref_r4_1d2b17'

def setup_inputs(seed: int=0):
    np.random.seed(seed)
    _w = jnp.asarray

    def _L0_attn_setup():
        import jax, jax.numpy as jnp
        import numpy as np
        HIDDEN = 1024
        HEAD_DIM = 128
        N_Q_HEADS = 32
        N_KV_HEADS = 8
        SLIDING_WINDOW = 256
        ROPE_THETA = 10000.0
        BATCH, SEQ = (1, 512)

        def _rope(t, pos):
            d = t.shape[-1]
            half = d // 2
            inv_freq = ROPE_THETA ** (-jnp.arange(half, dtype=jnp.float32) / half)
            ang = pos[:, None].astype(jnp.float32) * inv_freq[None, :]
            cos = jnp.cos(ang)[None, :, None, :]
            sin = jnp.sin(ang)[None, :, None, :]
            t1, t2 = (t[..., :half], t[..., half:])
            return jnp.concatenate([t1 * cos - t2 * sin, t1 * sin + t2 * cos], axis=-1)
        key = jax.random.key(seed)
        ks = jax.random.split(key, 5)
        w_scale = HIDDEN ** (-0.5)
        return {'x': jax.random.normal(ks[0], (BATCH, SEQ, HIDDEN), jnp.float32), 'wq': jax.random.normal(ks[1], (HIDDEN, N_Q_HEADS * HEAD_DIM), jnp.float32) * w_scale, 'wk': jax.random.normal(ks[2], (HIDDEN, N_KV_HEADS * HEAD_DIM), jnp.float32) * w_scale, 'wv': jax.random.normal(ks[3], (HIDDEN, N_KV_HEADS * HEAD_DIM), jnp.float32) * w_scale, 'wo': jax.random.normal(ks[4], (N_Q_HEADS * HEAD_DIM, HIDDEN), jnp.float32) * w_scale}
    _L0_attn_in = _L0_attn_setup()

    def _L0_ffn_setup():
        import jax, jax.numpy as jnp
        import numpy as np
        N_EXPERTS = 8
        TOP_K = 2
        D_MODEL = 1024
        RANK = 64
        key = jax.random.key(seed)
        k0, k1, k2, k3 = jax.random.split(key, 4)
        inputs = jax.random.normal(k0, (4, 512, D_MODEL), dtype=jnp.float32)
        gate_w = jax.random.normal(k1, (N_EXPERTS, D_MODEL), dtype=jnp.float32) * 0.02
        lora_A = jax.random.normal(k2, (N_EXPERTS, RANK, D_MODEL), dtype=jnp.float32) * 0.02
        lora_B = jax.random.normal(k3, (N_EXPERTS, D_MODEL, RANK), dtype=jnp.float32) * 0.02
        return {'inputs': inputs, 'gate_w': gate_w, 'lora_A': lora_A, 'lora_B': lora_B}
    _L0_ffn_in = _L0_ffn_setup()
    _L0_c = _w((lambda *s: np.random.randn(*s).astype(np.float32) * 0.05)(4, 1024))
    _L0_wmod = _w((lambda *s: np.random.randn(*s).astype(np.float32) * 0.05)(1024, 6 * 1024) * 1024 ** (-0.5))
    _d = {'L0_attn_x': _L0_attn_in['x'], 'L0_attn_wq': _L0_attn_in['wq'], 'L0_attn_wk': _L0_attn_in['wk'], 'L0_attn_wv': _L0_attn_in['wv'], 'L0_attn_wo': _L0_attn_in['wo'], 'L0_ffn_gate_w': _L0_ffn_in['gate_w'], 'L0_ffn_lora_A': _L0_ffn_in['lora_A'], 'L0_ffn_lora_B': _L0_ffn_in['lora_B'], 'L0_c': _L0_c, 'L0_wmod': _L0_wmod}
    _x0 = _d['L0_attn_x']
    _d['L0_attn_x'] = jax.random.normal(jax.random.fold_in(jax.random.key(seed), 1), (4, 512, 1024), dtype=_x0.dtype)
    del _x0
    return _d

def reference(L0_attn_x, L0_attn_wq, L0_attn_wk, L0_attn_wv, L0_attn_wo, L0_ffn_gate_w, L0_ffn_lora_A, L0_ffn_lora_B, L0_c, L0_wmod):

    def _L0_attn_ref(x, wq, wk, wv, wo):
        import jax, jax.numpy as jnp
        import numpy as np
        HIDDEN = 1024
        HEAD_DIM = 128
        N_Q_HEADS = 32
        N_KV_HEADS = 8
        SLIDING_WINDOW = 256
        ROPE_THETA = 10000.0
        BATCH, SEQ = (1, 512)

        def _rope(t, pos):
            d = t.shape[-1]
            half = d // 2
            inv_freq = ROPE_THETA ** (-jnp.arange(half, dtype=jnp.float32) / half)
            ang = pos[:, None].astype(jnp.float32) * inv_freq[None, :]
            cos = jnp.cos(ang)[None, :, None, :]
            sin = jnp.sin(ang)[None, :, None, :]
            t1, t2 = (t[..., :half], t[..., half:])
            return jnp.concatenate([t1 * cos - t2 * sin, t1 * sin + t2 * cos], axis=-1)
        B, S, _ = x.shape
        G = N_Q_HEADS // N_KV_HEADS
        sm_scale = HEAD_DIM ** (-0.5)
        q = (x @ wq).reshape(B, S, N_Q_HEADS, HEAD_DIM)
        k = (x @ wk).reshape(B, S, N_KV_HEADS, HEAD_DIM)
        v = (x @ wv).reshape(B, S, N_KV_HEADS, HEAD_DIM)
        pos = jnp.arange(S)
        q = _rope(q, pos)
        k = _rope(k, pos)
        qg = q.reshape(B, S, N_KV_HEADS, G, HEAD_DIM)
        scores = jnp.einsum('bqhgd,bshd->bhgqs', qg, k) * sm_scale
        i = pos[:, None]
        j = pos[None, :]
        allowed = (j <= i) & (j > i - SLIDING_WINDOW)
        neg = jnp.finfo(scores.dtype).min
        scores = jnp.where(allowed[None, None, None], scores, neg)
        attn = jax.nn.softmax(scores, axis=-1)
        out = jnp.einsum('bhgqs,bshd->bqhgd', attn, v).reshape(B, S, N_Q_HEADS * HEAD_DIM)
        return out @ wo

    def _L0_ffn_ref(inputs, gate_w, lora_A, lora_B):
        import jax, jax.numpy as jnp
        import numpy as np
        N_EXPERTS = 8
        TOP_K = 2
        D_MODEL = 1024
        RANK = 64
        x = inputs.reshape(-1, inputs.shape[-1])
        T = x.shape[0]
        gate_probs = jax.nn.softmax(x @ gate_w.T, axis=-1)
        weights, sel = jax.lax.top_k(gate_probs, TOP_K)
        weights = weights / jnp.sum(weights, axis=-1, keepdims=True)
        w_full = jnp.zeros((T, N_EXPERTS), dtype=x.dtype).at[jnp.arange(T)[:, None], sel].add(weights)
        out = jnp.zeros((T, D_MODEL), dtype=x.dtype)
        for e in range(N_EXPERTS):
            y = x @ lora_A[e].T @ lora_B[e].T
            out = out + w_full[:, e:e + 1] * y
        return out.reshape(inputs.shape[:-1] + (D_MODEL,))
    x = L0_attn_x
    mod = (_silu(L0_c) @ L0_wmod).reshape(L0_c.shape[0], 6, 1, -1)
    sa, ca, ga, sb, cb, gb = (mod[:, 0], mod[:, 1], mod[:, 2], mod[:, 3], mod[:, 4], mod[:, 5])
    ga = (2 * (ga >= 0) - 1) * jnp.maximum(jnp.abs(ga), 0.25)
    gb = (2 * (gb >= 0) - 1) * jnp.maximum(jnp.abs(gb), 0.25)
    h = _layernorm(x, axis=-1) * (1 + ca) + sa
    x = x + ga * _L0_attn_ref(h, L0_attn_wq, L0_attn_wk, L0_attn_wv, L0_attn_wo)
    h = _layernorm(x, axis=-1) * (1 + cb) + sb
    x = x + gb * _L0_ffn_ref(h, L0_ffn_gate_w, L0_ffn_lora_A, L0_ffn_lora_B)
    return x

_drawn_inputs = setup_inputs


def setup_inputs(seed=0):
    import zlib

    import numpy as np

    out = dict(_drawn_inputs(seed))
    spreads = {}
    factors = {'L0_ffn_gate_w': 3.524, 'L0_ffn_lora_A': 3.049, 'L0_ffn_lora_B': 3.055}
    for name, (base, spread) in spreads.items():
        noise = np.random.default_rng([zlib.crc32(name.encode()), seed]).standard_normal(out[name].shape)
        drawn = base * np.exp(spread * noise) if base else spread * noise
        out[name] = jnp.asarray(drawn.astype(out[name].dtype))
    for name, factor in factors.items():
        out[name] = (out[name] * factor).astype(out[name].dtype)
    return out
```

```python
from contextlib import ExitStack

import numpy as np

import concourse.bass as bass
from concourse import mybir

F32 = mybir.dt.float32
F32R = mybir.dt.float32r
U32 = mybir.dt.uint32
ALU = mybir.AluOpType
ACT = mybir.ActivationFunctionType

P = 128
BATCH, SEQ, D = 4, 512, 1024
HEADS, KV = 32, 8
GQ = HEADS // KV
HD = 128
WINDOW = 256
KT = D // P
QT = SEQ // P
UNITS = QT * GQ
SCALE = HD ** -0.5
EPS = 1e-5
E, R = 8, 64
ET = E * R // P
TILES = BATCH * QT
FAR = 3.0e38
NEG = -3.0e38
GROUPS = BATCH * KV
NC = 10
LA = 3


def key_tiles(i):
    return list(range(max(0, i - WINDOW // P), i + 1))


def constants():
    half = HD // 2
    inv = (np.float32(10000.0) ** (-np.arange(half, dtype=np.float32) / np.float32(half))).astype(np.float32)
    ang = inv[:, None] * np.arange(SEQ, dtype=np.float32)[None, :]
    cos, sin = np.cos(ang).astype(np.float32), np.sin(ang).astype(np.float32)
    p, j = np.arange(P)[:, None], np.arange(P)[None, :]
    mask = np.zeros((P, 3 * P), np.float32)
    mask[:, :P][~(j > p)] = NEG
    mask[:, 2 * P:][~(j <= p)] = NEG
    return {
        "cos": np.concatenate([cos, cos]),
        "sin": np.concatenate([-sin, sin]),
        "mask": mask,
        "ident": np.eye(P, dtype=np.float32),
        "iota": np.tile(np.arange(E, dtype=np.float32), (P, 1)),
    }


def adaln_block(nc, x, wq, wk, wv, wo, gate_w, lora_a, lora_b, c, wmod, cos, sin, mask, ident, iota, out):
    x_rows = x.rearrange("b s d -> (b s) d")
    out_rows = out.rearrange("b s d -> (b s) d")
    mod_d = nc.dram_tensor("mod_scratch", (6 * BATCH, D), F32, kind="Internal").ap()
    x1_d = nc.dram_tensor("x1_scratch", (BATCH * SEQ, D), F32, kind="Internal").ap()

    with ExitStack() as top:
        def sb(stack, name, shape, dt=F32):
            return stack.enter_context(nc.sbuf_tensor(name, shape, dt))

        def sem(name):
            return top.enter_context(nc.semaphore(name))

        bank = [top.enter_context(nc.psum_tensor(f"bank{i}", [P, 512], F32)) for i in range(8)]
        ident_t = sb(top, "ident_t", [P, P])
        modT = [sb(top, f"modT{l}", [P, BATCH, 2, KT]) for l in range(2)]
        modcur = sb(top, "modcur", [P, 2, 2, KT])
        barrier = sem("barrier")

        def plain(ins):
            return ins.wait_op(barrier, 5, "sem-ge")

        def phase_end(eng, k):
            eng.drain().then_inc(barrier, 1)
            eng.wait_ge(barrier, 5 * (k + 1))

        p0 = ExitStack()
        wm = [sb(p0, f"wm{i}", [P, KT, 512]) for i in range(2)]
        c_rows = sb(p0, "c_rows", [BATCH, D])
        c_sig = sb(p0, "c_sig", [BATCH, D])
        cT = sb(p0, "cT", [P, KT, BATCH])
        mrow = [sb(p0, f"mrow{i}", [BATCH, 512]) for i in range(2)]
        mabs = sb(p0, "mabs", [BATCH, 512])
        msgn = sb(p0, "msgn", [BATCH, 512])
        p0.close()
        NM = 6 * D // 512
        s_wm = [sem(f"s_wm{i}") for i in range(2)]
        s_c0 = sem("s_c0"); s_id = sem("s_id")
        s_sig = sem("s_sig"); s_v0 = sem("s_v0"); s_ct = sem("s_ct"); s_ctc = sem("s_ctc")
        s_mm0 = sem("s_mm0"); s_mr = sem("s_mr"); s_mt = sem("s_mt"); s_mc = sem("s_mc"); s_md = [sem("s_md0"), sem("s_md1")]

        def is_gate(j):
            return (j // 2) % 3 == 2

        def p0_sp(eng):
            eng.dma_start(ident_t[:], ident).then_inc(s_id, 16)
            eng.dma_start(c_rows[:], c).then_inc(s_c0, 16)
            for j in range(NM):
                if j >= 2:
                    eng.wait_ge(s_mm0, j - 1)
                eng.dma_start(wm[j % 2][:], wmod[:, j * 512:(j + 1) * 512].rearrange("(k p) n -> p k n", p=P)).then_inc(s_wm[j % 2], 16)

        def p0_act(eng):
            eng.wait_ge(s_c0, 16)
            eng.activation(c_sig[:], c_rows[:], ACT.Exp, scale=-1.0).then_inc(s_sig, 1)
            gates = 0
            for j in range(NM):
                eng.wait_ge(s_mm0, j + 1)
                if not is_gate(j):
                    if j >= 2 and not is_gate(j - 2):
                        eng.wait_ge(s_mt, sum(not is_gate(q) for q in range(j - 1)))
                    if j >= 2 and is_gate(j - 2):
                        eng.wait_ge(s_md[j % 2], 16 * sum(is_gate(q) for q in range(j % 2, j - 1, 2)))
                    eng.activation(mrow[j % 2][:], bank[j % 2][0:BATCH, :], ACT.Copy).then_inc(s_mr, 1)
                else:
                    eng.wait_ge(s_v0, v0_done[j])
                    q = j // 2 * BATCH
                    eng.dma_start(mod_d[q:q + BATCH, (j % 2) * 512:(j % 2 + 1) * 512], mrow[j % 2][:]).then_inc(s_md[j % 2], 16)
            for i in range(2):
                eng.wait_ge(s_md[i], 16 * sum(is_gate(q) for q in range(i, NM, 2)))

        v0_done, at = {}, 3
        for j in range(NM):
            at += 6 if is_gate(j) else 1
            v0_done[j] = at

        def p0_dve(eng):
            eng.wait_ge(s_sig, 1)
            eng.tensor_scalar(c_sig[:], c_sig[:], 1.0, None, ALU.add).then_inc(s_v0, 1)
            eng.wait_ge(s_v0, 1)
            eng.reciprocal(c_sig[:], c_sig[:]).then_inc(s_v0, 1)
            eng.wait_ge(s_v0, 2)
            eng.tensor_tensor(c_rows[:], c_rows[:], c_sig[:], ALU.mult).then_inc(s_v0, 1)
            eng.wait_ge(s_ct, 1)
            eng.tensor_copy(cT[:], bank[2][:, 0:KT * BATCH].rearrange("p (k b) -> p k b", b=BATCH)).then_inc(s_ctc, 1)
            turned = 0
            for j in range(NM):
                part, half = divmod(j, 2)
                if is_gate(j):
                    eng.wait_ge(s_mm0, j + 1)
                    if j >= 2 and not is_gate(j - 2):
                        eng.wait_ge(s_mt, turned)
                    v = v0_done[j] - 6
                    acc = bank[j % 2][0:BATCH, :]
                    steps = [
                        lambda: eng.tensor_scalar(mabs[:], acc, -1.0, None, ALU.mult),
                        lambda: eng.tensor_tensor(mabs[:], mabs[:], acc, ALU.max),
                        lambda: eng.tensor_scalar(mabs[:], mabs[:], 0.25, None, ALU.max),
                        lambda: eng.tensor_scalar(msgn[:], acc, 0.0, 2.0, ALU.is_ge, ALU.mult),
                        lambda: eng.tensor_scalar(msgn[:], msgn[:], -1.0, None, ALU.add),
                        lambda: eng.tensor_tensor(mrow[j % 2][:], msgn[:], mabs[:], ALU.mult),
                    ]
                    for n, step in enumerate(steps):
                        eng.wait_ge(s_v0, v + n)
                        step().then_inc(s_v0, 1)
                else:
                    turned += 1
                    eng.wait_ge(s_mt, turned)
                    src = bank[2 + turned % 2][:, 0:4 * BATCH].rearrange("p (k b) -> p b k", b=BATCH)
                    dst = modT[part // 3][:, :, part % 3, half * 4:half * 4 + 4]
                    eng.tensor_scalar(dst, src, float(part % 3), None, ALU.add).then_inc(s_v0, 1)
            eng.wait_ge(s_v0, v0_done[NM - 1])

        def p0_pe(eng):
            eng.wait_ge(s_id, 16)
            eng.wait_ge(s_v0, 3)
            for k in range(KT):
                m = eng.transpose(bank[2][:, k * BATCH:(k + 1) * BATCH], c_rows[:, k * P:(k + 1) * P], ident_t[0:BATCH, 0:BATCH])
            m.then_inc(s_ct, 1)
            eng.wait_ge(s_ctc, 1)
            turned = 0

            def turn(j):
                nonlocal turned
                if is_gate(j):
                    return
                turned += 1
                eng.wait_ge(s_mr, turned)
                if turned >= 3:
                    prev = [q for q in range(NM) if not is_gate(q)][turned - 3]
                    eng.wait_ge(s_v0, v0_done[prev])
                for k in range(4):
                    m = eng.transpose(bank[2 + turned % 2][:, k * BATCH:(k + 1) * BATCH], mrow[j % 2][:, k * P:(k + 1) * P],
                                      ident_t[0:BATCH, 0:BATCH])
                m.then_inc(s_mt, 1)

            for j in range(NM):
                eng.wait_ge(s_wm[j % 2], 16 * (j // 2 + 1))
                if j >= 2:
                    if is_gate(j - 2):
                        eng.wait_ge(s_v0, v0_done[j - 2])
                    else:
                        eng.wait_ge(s_mr, sum(not is_gate(q) for q in range(j - 1)))
                for k in range(KT):
                    m = eng.matmul(bank[j % 2][0:BATCH, :], cT[:, k, :], wm[j % 2][:, k, :], start=k == 0, stop=k == KT - 1)
                m.then_inc(s_mm0, 1)
                if j:
                    turn(j - 1)
            turn(NM - 1)

        p1 = ExitStack()

        def split_pair(stack, name, shape):
            return sb(stack, name + "_hi", shape, F32R), sb(stack, name + "_lo", shape, F32R)

        hT = split_pair(p1, "hT", [P, KT, SEQ])
        acc = sb(p1, "acc", [P, QT, D])
        w_q = split_pair(p1, "w_q", [P, KT, GQ * HD])
        w_k = split_pair(p1, "w_k", [P, KT, HD])
        w_v = split_pair(p1, "w_v", [P, KT, HD])
        w_o = split_pair(p1, "w_o", [P, GQ, D])
        stage = [sb(p1, f"stage{i}", [P, 1024]) for i in range(2)]
        qo = split_pair(p1, "qo", [P, GQ, SEQ])
        kt_ = split_pair(p1, "kt_", [P, SEQ])
        v_ = split_pair(p1, "v_", [P, QT, HD])
        swapped = [sb(p1, f"swapped{i}", [P, SEQ]) for i in range(2)]
        rotated = [sb(p1, f"rotated{i}", [P, SEQ]) for i in range(2)]
        prob = sb(p1, "prob", [P, GQ, 3 * P])
        cos_t = sb(p1, "cos_t", [P, SEQ])
        sin_t = sb(p1, "sin_t", [P, SEQ])
        mask_t = sb(p1, "mask_t", [P, 3 * P])
        nbias = sb(p1, "nbias", [P, UNITS])
        rowsum = sb(p1, "rowsum", [P, UNITS])
        rrow = sb(p1, "rrow", [P, UNITS])
        stats = sb(p1, "stats", [P, QT, 2, 6])
        mv = sb(p1, "mv", [P, QT, 2])
        lnv = sb(p1, "lnv", [P, 6, QT])
        with ExitStack() as a:
            pT = [split_pair(a, f"pT{i}", [P, 3, GQ * P]) for i in range(2)]
        with ExitStack() as a:
            xb = sb(a, "xb", [P, QT, D])
            ga_t = sb(a, "ga_t", [P, D])
        p1.close()

        s_cst = sem("s_cst")
        s_stage = [sem("s_stage0"), sem("s_stage1")]
        s_split = sem("s_split")
        s_proj = sem("s_proj")
        s_wo = sem("s_wo")
        s_act = sem("s_act")
        s_dve = sem("s_dve")
        s_swp = sem("s_swp"); s_rs = sem("s_rs"); s_ra = sem("s_ra"); s_rh = sem("s_rh")
        s_qk = sem("s_qk")
        s_vt = sem("s_vt"); s_vh = sem("s_vh"); s_v = sem("s_v")
        s_S = sem("s_S"); s_msk = sem("s_msk"); s_exp = sem("s_exp"); s_rl = sem("s_rl"); s_nrm = sem("s_nrm")
        s_T = sem("s_T"); s_pth = sem("s_pth"); s_ptl = sem("s_ptl"); s_pv = sem("s_pv"); s_oh = sem("s_oh"); s_ol = sem("s_ol")
        s_xb = [sem(f"s_xb{t}") for t in range(QT)]
        s_ga = sem("s_ga"); s_x1 = sem("s_x1")
        s_ln = sem("s_ln"); s_sq = sem("s_sq"); s_xn = sem("s_xn"); s_lnT = sem("s_lnT"); s_lna = sem("s_lna"); s_lnh = sem("s_lnh"); s_h = sem("s_h")
        s_fin = sem("s_fin"); s_acc0 = sem("s_acc0"); s_mc1 = sem("s_mc1")

        LN_STEPS = 3 * QT + 8
        s_wor = sem("s_wor")

        def bank_free(eng, n, name):
            before = {"wo1": 1, "Q1": 1, "Q2": 2, "Q3": 3, "V": 4, "VT": 5}
            if name in before:
                eng.wait_ge(s_rs, 5 * n + before[name])

        def chunk_source(j, g):
            if j == 0 or j == 5:
                w = wv if j == 0 else wk
                return w[:, bass.ds(g * HD, HD)].rearrange("(k p) n -> p k n", p=P), "p (k n) -> p k n", dict(n=HD)
            if j <= 4:
                k = 2 * (j - 1)
                return wq[k * P:(k + 2) * P, bass.ds(g * GQ * HD, GQ * HD)].rearrange("(k p) n -> p k n", p=P), "p (k n) -> p k n", dict(k=2)
            return wo[bass.ds(g * GQ * HD + (j - 6) * HD, HD), :], None, None

        def load_chunk(eng, slot, j, g):
            src, pat, kw = chunk_source(j, g)
            dst = stage[slot][:]
            if pat:
                dst = dst.rearrange(pat, **kw)
            eng.dma_start(dst, src).then_inc(s_stage[slot], 16)

        def p1_sp(eng):
            for t, src in ((cos_t, cos), (sin_t, sin), (mask_t, mask)):
                eng.dma_start(t[:], src).then_inc(s_cst, 16)
            load_chunk(eng, 0, 5, 0)
            with eng.Fori(0, GROUPS) as n:
                for j in range(NC):
                    eng.wait_ge(s_split, 10 * n + j + 1)
                    load_chunk(eng, (1 + j) % 2, j, (n + 1) % KV if j == 5 else n % KV)

        def split_chunk(eng, slot, dst, load_no, base):
            eng.wait_ge(s_stage[slot], 16 * load_no)
            hi, lo = dst
            src = stage[slot][:]
            if len(hi.shape) == 3:
                src = src.rearrange("p (k n) -> p k n", n=hi.shape[2])
            plain(eng.tensor_copy(hi, src)).then_inc(s_hi, 1)
            eng.wait_ge(s_hi, base)
            eng.tensor_tensor(lo, src, hi.bitcast(F32), ALU.subtract).then_inc(s_split, 1)

        s_hi = sem("s_hi")

        def p1_pool(eng):
            eng.sem_inc(s_split, 1)
            split_chunk(eng, 0, (w_k[0][:], w_k[1][:]), 1, 1)
            with eng.Fori(0, GROUPS) as n:
                eng.wait_ge(s_proj, 6 * n + 1)
                for j in range(NC):
                    slot = (1 + j) % 2
                    if j == 0:
                        dst = tuple(w[:] for w in w_v)
                    elif j <= 4:
                        dst = tuple(w[:, 2 * (j - 1):2 * j, :] for w in w_q)
                    elif j == 5:
                        eng.wait_ge(s_proj, 6 * n + 2)
                        dst = tuple(w[:] for w in w_k)
                    else:
                        if j == 6:
                            eng.wait_ge(s_wo, 8 * n + 1)
                        dst = tuple(w[:, j - 6, :] for w in w_o)
                    split_chunk(eng, slot, dst, 5 * n + (1 + j) // 2 + 1, 10 * n + j + 2)
                for u in range(UNITS):
                    w = P * len(key_tiles(u // GQ))
                    eng.wait_ge(s_rl, UNITS * n + u + 1)
                    tile = prob[:, u % GQ, 0:w]
                    plain(eng.tensor_scalar(tile, tile, rrow[:, u:u + 1], None, ALU.mult)).then_inc(s_nrm, 1)

        def mm3(eng, o, st, mv_, start, stop):
            eng.matmul(o, st[0], mv_[0], start=start, stop=False)
            eng.matmul(o, st[0], mv_[1], start=False, stop=False)
            return eng.matmul(o, st[1], mv_[0], start=False, stop=stop)

        def sl(pair, f):
            return tuple(f(t) for t in pair)

        def pe_project(eng, n, name, w, cols, bk, waits):
            bank_free(eng, n, name)
            for k in range(KT):
                if k in waits:
                    eng.wait_ge(*waits[k])
                m = mm3(eng, bank[bk][:], sl(w, lambda t: t[:, k, cols]), sl(hT, lambda t: t[:, k, :]), k == 0, k == KT - 1)
            m.then_inc(s_proj, 1)

        def pe_wo(eng, n, half, first_of_bank):
            t, c = divmod(half, 2)
            if half == 0:
                eng.wait_ge(s_ol, QT * n + QT)
            if half >= 2:
                eng.wait_ge(s_wor, 8 * n + half)
            elif first_of_bank is not None:
                first_of_bank(half)
            for h in range(GQ):
                m = mm3(eng, bank[1 - half % 2][:], sl(qo, lambda q: q[:, h, t * P:(t + 1) * P]),
                        sl(w_o, lambda w: w[:, h, c * 512:(c + 1) * 512]), h == 0, h == GQ - 1)
            m.then_inc(s_wo, 1)

        def pe_scores(eng, n, u):
            i, h = divmod(u, GQ)
            kts = key_tiles(i)
            if i == 0:
                eng.wait_ge(s_qk, 5 * n + 2 + h)
            if u >= 3:
                eng.wait_ge(s_msk, UNITS * n + u - 2)
            mm3(eng, bank[2 + u % 3][:, 0:P * len(kts)], sl(qo, lambda q: q[:, h, i * P:(i + 1) * P]),
                sl(kt_, lambda k: k[:, kts[0] * P:(i + 1) * P]), True, True).then_inc(s_S, 1)

        def pe_turn(eng, n, u):
            eng.wait_ge(s_nrm, UNITS * n + u + 1)
            if u >= 2:
                eng.wait_ge(s_ptl, UNITS * n + u - 1)
            for b in range(len(key_tiles(u // GQ))):
                m = eng.transpose(bank[5 + u % 2][:, b * P:(b + 1) * P], prob[:, u % GQ, b * P:(b + 1) * P], ident_t[:])
            m.then_inc(s_T, 1)

        def pe_values(eng, n, i):
            eng.wait_ge(s_ptl, UNITS * n + GQ * (i + 1))
            if i == 0:
                eng.wait_ge(s_v, n + 2)
            else:
                eng.wait_ge(s_ol, QT * n + i)
            kts = key_tiles(i)
            for b, kt in enumerate(kts):
                m = mm3(eng, bank[7][:], sl(v_, lambda v: v[:, kt, :]), sl(pT[i % 2], lambda p: p[:, b, :]), b == 0, b == len(kts) - 1)
            m.then_inc(s_pv, 1)

        def pe_attention(eng, n):
            for u in range(LA):
                pe_scores(eng, n, u)
            bank_free(eng, n, "VT")
            eng.wait_ge(s_act, 7 * n + 6)
            for t in range(QT):
                m = eng.transpose(bank[0][:, t * P:(t + 1) * P], swapped[1][:, t * P:(t + 1) * P], ident_t[:])
            m.then_inc(s_vt, 1)
            for u in range(UNITS):
                if u + LA < UNITS:
                    pe_scores(eng, n, u + LA)
                pe_turn(eng, n, u)
                if u % GQ == 1 and u > GQ:
                    pe_values(eng, n, u // GQ - 1)
            pe_values(eng, n, QT - 1)

        def pe_k(eng, n, b=None):
            waits = {0: (s_split, 10 * n + 2)}
            if b is None:
                pe_project(eng, n, "K", w_k, slice(0, HD), 0, waits)
                return
            eng.wait_ge(s_wor, 8 * n + 1)
            eng.wait_ge(*waits[0])
            for k in range(KT):
                eng.wait_ge(s_h, KT * b + k + 1)
                m = mm3(eng, bank[0][:], sl(w_k, lambda t: t[:, k, :]), sl(hT, lambda t: t[:, k, :]), k == 0, k == KT - 1)
            m.then_inc(s_proj, 1)

        def pe_qv(eng, n):
            for h in range(GQ):
                waits = {2 * q: (s_split, 10 * n + 4 + q) for q in range(4)} if h == 0 else {}
                pe_project(eng, n, f"Q{h}", w_q, slice(h * HD, (h + 1) * HD), 1 - h % 2, waits)
            pe_project(eng, n, "V", w_v, slice(0, HD), 1, {})

        def pe_ln_turn(eng, b1, m_):
            for k in range(KT):
                if k == 0:
                    eng.wait_ge(s_xn, QT * b1 + QT)
                if k >= 2:
                    eng.wait_ge(s_lna, KT * b1 + k - 1)
                for t in range(QT):
                    m = eng.transpose(bank[2 + k % 2][:, t * P:(t + 1) * P], xb[:, t, k * P:(k + 1) * P], ident_t[:])
                m.then_inc(s_lnT, 1)

        def p1_pe(eng):
            eng.sem_inc(s_proj, 1)
            eng.sem_inc(s_wo, 1)
            pe_ln_turn(eng, 0, None)
            with eng.Fori(0, BATCH) as b:
                pe_k(eng, KV * b, b)
                pe_qv(eng, KV * b)
                pe_attention(eng, KV * b)
                with eng.Fori(1, KV) as g:
                    n = b * KV + g
                    pe_k(eng, n)
                    for half in range(8):
                        pe_wo(eng, n - 1, half, lambda hf: bank_free(eng, n, f"wo{hf}"))
                    eng.wait_ge(s_wor, 8 * n + 1)
                    pe_qv(eng, n)
                    pe_attention(eng, n)
                n = b * KV + (KV - 1)
                for half in range(6):
                    pe_wo(eng, n, half, None)
                pe_ln_turn(eng, b + 1, None)
                for half in range(6, 8):
                    pe_wo(eng, n, half, None)

        def act_rope(eng, n, r, name):
            slot = r % 2
            eng.wait_ge(s_dve, 5 * n + r + 1)
            if r >= 2:
                eng.wait_ge(s_qk, 5 * n + r - 1)
            half = HD // 2
            bk = bank[0 if r % 2 == 0 else 1]
            eng.activation(swapped[slot][0:half, :], bk[half:HD, :], ACT.Copy)
            eng.activation(swapped[slot][half:HD, :], bk[0:half, :], ACT.Copy).then_inc(s_act, 1)
            dst = kt_[0][:] if r == 0 else qo[0][:, r - 1, :]
            eng.wait_ge(s_ra, 5 * n + r + 1)
            eng.activation(dst, rotated[slot][:], ACT.Copy).then_inc(s_rh, 1)

        def act_attention(eng, n, first):
            eng.wait_ge(s_proj, 6 * n + 7)
            eng.wait_ge(s_qk, 5 * n + 4)
            eng.activation(swapped[1][:], bank[1][:], ACT.Copy).then_inc(s_act, 1)
            for s in range(UNITS + LA + 5):
                if s == 2:
                    eng.wait_ge(s_vt, n + 1)
                    eng.activation(v_[0][:], bank[0][:].rearrange("p (t d) -> p t d", d=HD), ACT.Copy).then_inc(s_act, 1)
                if s < UNITS:
                    w = P * len(key_tiles(s // GQ))
                    tile = prob[:, s % GQ, 0:w]
                    eng.wait_ge(s_msk, UNITS * n + s + 1)
                    eng.activation(tile, tile, ACT.Exp, bias=nbias[:, s:s + 1], scale=-1.0,
                                   accum_out=rowsum[:, s:s + 1]).then_inc(s_exp, 1)
                u = s - LA - 1
                if 0 <= u < UNITS:
                    i, h = divmod(u, GQ)
                    eng.wait_ge(s_T, UNITS * n + u + 1)
                    if h == 0 and i >= 2:
                        eng.wait_ge(s_pv, QT * n + i - 1)
                    if u == 0 and first is not None:
                        eng.wait_ge(s_x1, 16 * QT * first + 16)
                    nk = len(key_tiles(i))
                    eng.activation(pT[i % 2][0][:, 0:nk, h * P:(h + 1) * P],
                                   bank[5 + u % 2][:, 0:nk * P].rearrange("p (b q) -> p b q", q=P), ACT.Copy).then_inc(s_pth, 1)
                if s >= 10 and (s - 10) % GQ == 0 and (s - 10) // GQ < QT - 1:
                    act_outputs(eng, n, (s - 10) // GQ)
            act_outputs(eng, n, QT - 1)

        def act_outputs(eng, n, i):
            eng.wait_ge(s_pv, QT * n + i + 1)
            eng.activation(qo[0][:, :, i * P:(i + 1) * P], bank[7][:].rearrange("p (h q) -> p h q", q=P), ACT.Copy).then_inc(s_oh, 1)

        def act_load_x(eng, b, tiles):
            for t in tiles:
                eng.dma_start(xb[:, t, :], x_rows[bass.ds(b * SEQ + t * P, P), :]).then_inc(s_xb[t], 16)

        def act_ln(eng, b1):
            eng.wait_ge(s_ln, LN_STEPS * b1 + LN_VAR)
            eng.activation(lnv[:, 1, :], lnv[:, 0, :], ACT.Sqrt).then_inc(s_sq, 1)
            for k in range(KT):
                eng.wait_ge(s_lnT, KT * b1 + k + 1)
                if k == 0:
                    eng.wait_ge(s_mc1, b1 + 1)
                if k >= 2:
                    eng.wait_ge(s_h, KT * b1 + k - 1)
                eng.activation(rotated[k % 2][:], bank[2 + k % 2][:], ACT.Identity, bias=modcur[:, 0, 0, k:k + 1],
                               scale=modcur[:, 0, 1, k:k + 1]).then_inc(s_lna, 1)
                eng.wait_ge(s_lna, KT * b1 + k + 1)
                eng.activation(hT[0][:, k, :], rotated[k % 2][:], ACT.Copy).then_inc(s_lnh, 1)

        def p1_act(eng):
            eng.sem_inc(s_x1, 16)
            act_load_x(eng, 0, range(QT))
            act_ln(eng, 0)
            with eng.Fori(0, BATCH) as b:
                for r in range(1 + GQ):
                    act_rope(eng, KV * b, r, None)
                act_attention(eng, KV * b, b)
                with eng.Fori(1, KV) as g:
                    n = b * KV + g
                    for r in range(1 + GQ):
                        act_rope(eng, n, r, None)
                    act_attention(eng, n, None)
                n = b * KV + (KV - 1)
                act_load_x(eng, (b + 1) % BATCH, range(QT))
                eng.dma_start(ga_t[:], mod_d[bass.ds(2 * BATCH + b, 1), :].partition_broadcast(P) if False else
                              mod_d[bass.ds(2 * BATCH + b, 1), :].broadcast_to([P, D])).then_inc(s_ga, 16)
                act_ln(eng, b + 1)
                act_load_x(eng, b, range(QT))
                for t in range(QT):
                    eng.wait_ge(s_fin, 2 * QT * b + 2 * t + 2)
                    eng.dma_start(x1_d[bass.ds(b * SEQ + t * P, P), :], xb[:, t, :]).then_inc(s_x1, 16)
            eng.wait_ge(s_x1, 16 * TILES + 16)

        LN_VAR = 3 * QT + 1

        def dve_rope(eng, n, r):
            slot = r % 2
            bk = bank[0 if r % 2 == 0 else 1]
            eng.wait_ge(s_proj, 6 * n + 2 + r)
            eng.tensor_tensor(rotated[slot][:], bk[:], cos_t[:], ALU.mult).then_inc(s_dve, 1)
            eng.wait_ge(s_act, 7 * n + r + 1)
            eng.tensor_tensor(swapped[slot][:], swapped[slot][:], sin_t[:], ALU.mult).then_inc(s_rs, 1)
            eng.wait_ge(s_rs, 5 * n + r + 1)
            eng.wait_ge(s_dve, 5 * n + r + 1)
            eng.tensor_tensor(rotated[slot][:], rotated[slot][:], swapped[slot][:], ALU.add).then_inc(s_ra, 1)
            eng.wait_ge(s_rh, 5 * n + r + 1)
            eng.wait_ge(s_ra, 5 * n + r + 1)
            hi, lo = (kt_[0][:], kt_[1][:]) if r == 0 else (qo[0][:, r - 1, :], qo[1][:, r - 1, :])
            eng.tensor_tensor(lo, rotated[slot][:], hi.bitcast(F32), ALU.subtract).then_inc(s_qk, 1)

        def dve_wo(eng, n, half):
            t, cc = divmod(half, 2)
            eng.wait_ge(s_wo, 8 * n + half + 2)
            a = acc[:, t, cc * 512:(cc + 1) * 512]
            eng.tensor_tensor(a, bank[1 - half % 2][:], a, ALU.add).then_inc(s_wor, 1)

        def dve_outputs(eng, n, i):
            eng.wait_ge(s_oh, QT * n + i + 1)
            o = bank[7][:].rearrange("p (h q) -> p h q", q=P)
            eng.tensor_tensor(qo[1][:, :, i * P:(i + 1) * P], o, qo[0][:, :, i * P:(i + 1) * P].bitcast(F32),
                              ALU.subtract).then_inc(s_ol, 1)

        def dve_attention(eng, n):
            for s in range(UNITS + LA + 5):
                if s == 2:
                    eng.wait_ge(s_act, 7 * n + 7)
                    eng.tensor_tensor(v_[1][:], bank[0][:].rearrange("p (t d) -> p t d", d=HD), v_[0][:].bitcast(F32),
                                      ALU.subtract).then_inc(s_v, 1)
                if s < UNITS:
                    w = P * len(key_tiles(s // GQ))
                    eng.wait_ge(s_S, UNITS * n + s + 1)
                    if s >= GQ:
                        eng.wait_ge(s_T, UNITS * n + s - GQ + 1)
                    plain(eng.tensor_tensor_reduce(prob[:, s % GQ, 0:w], bank[2 + s % 3][:, 0:w], mask_t[:, 3 * P - w:3 * P], -SCALE, FAR,
                                             ALU.add, ALU.min, nbias[:, s:s + 1])).then_inc(s_msk, 1)
                if 1 <= s < UNITS + 1:
                    eng.wait_ge(s_exp, UNITS * n + s)
                    eng.reciprocal(rrow[:, s - 1:s], rowsum[:, s - 1:s]).then_inc(s_rl, 1)
                u = s - LA - 1
                if 0 <= u < UNITS:
                    i, h = divmod(u, GQ)
                    nk = len(key_tiles(i))
                    eng.wait_ge(s_pth, UNITS * n + u + 1)
                    hi, lo = (p[:, 0:nk, h * P:(h + 1) * P] for p in pT[i % 2])
                    eng.tensor_tensor(lo, bank[5 + u % 2][:, 0:nk * P].rearrange("p (b q) -> p b q", q=P), hi.bitcast(F32),
                                      ALU.subtract).then_inc(s_ptl, 1)
                if s >= 10 and (s - 10) % GQ == 0 and (s - 10) // GQ < QT - 1:
                    dve_outputs(eng, n, (s - 10) // GQ)
            dve_outputs(eng, n, QT - 1)

        def ln_ops(eng, xt, st, mv_, lv, steps, base, semaphore, ntile, wait_x, wait_sq, fill):
            cnt = [0]

            def do(ins):
                cnt[0] += 1
                ins.then_inc(semaphore, 1)

            def after():
                eng.wait_ge(semaphore, base + cnt[0])

            for t in range(ntile):
                wait_x(t)
                do(plain(eng.bn_stats(st[:, t, 0, :], xt(t)[:, 0:512])))
                do(eng.bn_stats(st[:, t, 1, :], xt(t)[:, 512:1024]))
                after()
                do(plain(eng.bn_aggr(mv_[:, t, :], st[:, t, :, :].rearrange("p a s -> p (a s)"))))
                fill(t)
            after()
            do(eng.tensor_scalar(lv[:, 0, :], mv_[:, :, 1], EPS, None, ALU.add))
            wait_sq()
            do(eng.reciprocal(lv[:, 1, :], lv[:, 1, :])); after()
            do(eng.tensor_tensor(lv[:, 2, :], lv[:, 1, :], lv[:, 1, :], ALU.mult)); after()
            do(eng.tensor_tensor(lv[:, 2, :], lv[:, 2, :], lv[:, 0, :], ALU.mult)); after()
            do(eng.tensor_scalar(lv[:, 2, :], lv[:, 2, :], -0.5, 1.5, ALU.mult, ALU.add)); after()
            do(eng.tensor_tensor(lv[:, 3, :], lv[:, 2, :], lv[:, 1, :], ALU.mult)); after()
            do(eng.tensor_scalar(lv[:, 4, :], mv_[:, :, 0], -1.0, None, ALU.mult)); after()
            do(eng.tensor_tensor(lv[:, 5, :], lv[:, 4, :], lv[:, 3, :], ALU.mult)); after()
            assert cnt[0] == steps, cnt

        def dve_ln(eng, b1, b, xloads, fill, fill2):
            eng.tensor_copy(modcur[:, 0, :, :], modT[0][:, bass.ds(b, 1), :, :].rearrange("p o s k -> p (o s) k")).then_inc(s_mc1, 1)
            ln_ops(eng, lambda t: xb[:, t, :], stats, mv, lnv, LN_STEPS, LN_STEPS * b1, s_ln, QT,
                   lambda t: eng.wait_ge(s_xb[t], 16 * xloads), lambda: eng.wait_ge(s_sq, b1 + 1), fill)
            for t in range(QT):
                eng.tensor_scalar(xb[:, t, :], xb[:, t, :], lnv[:, 3, t:t + 1], lnv[:, 5, t:t + 1], ALU.mult, ALU.add).then_inc(s_xn, 1)
            fill2()
            for k in range(KT):
                eng.wait_ge(s_lnh, KT * b1 + k + 1)
                eng.tensor_tensor(hT[1][:, k, :], rotated[k % 2][:], hT[0][:, k, :].bitcast(F32), ALU.subtract).then_inc(s_h, 1)

        def p1_dve(eng):
            eng.sem_inc(s_v, 1)
            eng.sem_inc(s_wor, 1)
            eng.memset(acc[:], 0.0).then_inc(s_acc0, 1)
            eng.wait_ge(s_cst, 48)
            dve_ln(eng, 0, 0, 1, lambda t: None, lambda: None)
            with eng.Fori(0, BATCH) as b:
                for r in range(1 + GQ):
                    dve_rope(eng, KV * b, r)
                dve_attention(eng, KV * b)
                with eng.Fori(1, KV) as g:
                    n = b * KV + g
                    dve_rope(eng, n, 0)
                    eng.wait_ge(s_acc0, b + 1)
                    for half in range(8):
                        dve_wo(eng, n - 1, half)
                    for r in range(1, 1 + GQ):
                        dve_rope(eng, n, r)
                    dve_attention(eng, n)
                n = b * KV + (KV - 1)

                def fill2():
                    dve_wo(eng, n, 4)
                    dve_wo(eng, n, 5)
                dve_ln(eng, b + 1, (b + 1) % BATCH, 2 * b + 2, lambda t: dve_wo(eng, n, t), fill2)
                dve_wo(eng, n, 6)
                dve_wo(eng, n, 7)
                eng.wait_ge(s_ga, 16 * b + 16)
                eng.wait_ge(s_wor, 8 * n + 9)
                for t in range(QT):
                    eng.tensor_tensor(acc[:, t, :], acc[:, t, :], ga_t[:], ALU.mult).then_inc(s_fin, 1)
                    eng.wait_ge(s_fin, 2 * QT * b + 2 * t + 1)
                    eng.wait_ge(s_xb[t], 16 * (2 * b + 3))
                    eng.tensor_tensor(xb[:, t, :], xb[:, t, :], acc[:, t, :], ALU.add).then_inc(s_fin, 1)
                eng.wait_ge(s_fin, 2 * QT * b + 2 * QT)
                eng.memset(acc[:], 0.0).then_inc(s_acc0, 1)

        p2 = ExitStack()
        SLOTS = 4

        def tile_slot(buf, t):
            return buf[:, bass.ds(t % SLOTS, 1), :].rearrange("p o d -> p (o d)")

        aT = split_pair(p2, "aT", [P, KT, E * R])
        bT = split_pair(p2, "bT", [P, ET, D])
        gT = split_pair(p2, "gT", [P, KT, E])
        h2 = [split_pair(p2, f"h2{i}", [P, KT, P]) for i in range(2)]
        hf = sb(p2, "hf", [P, KT, P])
        x1 = sb(p2, "x1", [P, SLOTS, D])
        xn2 = sb(p2, "xn2", [P, D])
        gb = sb(p2, "gb", [P, SLOTS, D])
        us = sb(p2, "us", [P, E, R])
        usT = split_pair(p2, "usT", [P, ET, P])
        yo = sb(p2, "yo", [P, D])
        st2 = sb(p2, "st2", [P, 1, 2, 6])
        mv2 = sb(p2, "mv2", [P, 1, 2])
        lnv2 = sb(p2, "lnv2", [P, 6, 1])
        logit = sb(p2, "logit", [P, E])
        top8 = sb(p2, "top8", [P, E])
        idx8 = sb(p2, "idx8", [P, E], U32)
        idxf = sb(p2, "idxf", [P, E])
        gv = sb(p2, "gv", [P, 8])
        oneh = sb(p2, "oneh", [P, 2, E])
        wfull = sb(p2, "wfull", [P, E])
        iota_t = sb(p2, "iota_t", [P, E])
        a_in = sb(p2, "a_in", [P, ET, D])
        b_in = sb(p2, "b_in", [P, KT, E, R])
        g_in = sb(p2, "g_in", [E, D])
        p2.close()

        t_in = sem("t_in"); t_T = sem("t_T"); t_hi = sem("t_hi"); t_lo = sem("t_lo")
        t_x1 = [sem("t_x10"), sem("t_x11")]; t_gb = [sem("t_gb0"), sem("t_gb1")]
        t_ln = sem("t_ln"); t_sq = sem("t_sq"); t_xn = sem("t_xn"); t_hT = sem("t_hT"); t_aff = sem("t_aff")
        t_h2h = sem("t_h2h"); t_h2 = sem("t_h2"); t_mc = sem("t_mc")
        t_U = sem("t_U"); t_G = sem("t_G"); t_gate = sem("t_gate"); t_e = sem("t_e"); t_us = sem("t_us"); t_UT = sem("t_UT")
        t_uh = sem("t_uh"); t_ul = sem("t_ul"); t_Y = sem("t_Y"); t_y = sem("t_y"); t_out = sem("t_out")
        NTURN = KT + 2 * ET + 1
        LN2_STEPS = 3 + 8
        GATE = 9

        def turned_weights():
            for k in range(KT):
                yield [a_in[:, cc, k * P:(k + 1) * P] for cc in range(ET)], sl(aT, lambda a: a[:, k, :]), P
            for cc in range(ET):
                for half in range(2):
                    yield [b_in[:, 4 * half + j, 2 * cc:2 * cc + 2, :].rearrange("p e r -> p (e r)") for j in range(4)], \
                        sl(bT, lambda w: w[:, cc, half * 512:(half + 1) * 512]), P
            yield [g_in[:, k * P:(k + 1) * P] for k in range(KT)], sl(gT, lambda g: g[:].rearrange("p k e -> p (k e)")), E

        def p2_sp(eng):
            eng.dma_start(a_in[:], lora_a.rearrange("(c e) r d -> (e r) c d", e=2)).then_inc(t_in, 16)
            for e in range(E):
                eng.dma_start(b_in[:, :, e, :], lora_b[e].rearrange("(k p) r -> p k r", p=P)).then_inc(t_in, 16)
            eng.dma_start(g_in[:], gate_w).then_inc(t_in, 16)
            eng.dma_start(iota_t[:], iota).then_inc(t_in, 16)

        T_IN = 16 * (3 + E)

        def p2_load(eng, t, slot):
            eng.dma_start(tile_slot(x1, t), x1_d[bass.ds(t % TILES * P, P), :]).then_inc(t_x1[slot], 16)
            eng.dma_start(tile_slot(gb, t), mod_d[bass.ds(5 * BATCH + t % TILES // QT, 1), :].broadcast_to([P, D])).then_inc(t_gb[slot], 16)

        def tile_pairs(eng, body):
            with eng.Fori(0, TILES // 2 - 1) as q:
                for z in range(2):
                    body(2 * q + 1 + z, (1 + z) % 2, q + (1 if z == 0 else 2))

        def p2_act_ln(eng, t, slot):
            eng.wait_ge(t_ln, LN2_STEPS * t + 4)
            eng.activation(lnv2[:, 1, :], lnv2[:, 0, :], ACT.Sqrt).then_inc(t_sq, 1)

        def p2_act_h(eng, t, slot):
            for half in range(2):
                eng.wait_ge(t_hT, 2 * t + half + 1)
                if half == 0:
                    eng.wait_ge(t_mc, t + 1)
                    eng.wait_ge(t_h2, t + 1)
                for k in range(4 * half, 4 * half + 4):
                    ins = eng.activation(hf[:, k, :], bank[6 + half][:, (k % 4) * P:(k % 4 + 1) * P], ACT.Identity,
                                         bias=modcur[:, 1, 0, k:k + 1], scale=modcur[:, 1, 1, k:k + 1])
                ins.then_inc(t_aff, 1)
            eng.wait_ge(t_aff, 2 * t + 2)
            eng.activation(h2[slot][0][:], hf[:], ACT.Copy).then_inc(t_h2h, 1)

        def p2_act_mid(eng, t):
            eng.wait_ge(t_gate, GATE * t + 4)
            eng.activation(gv[:, 1:2], gv[:, 0:1], ACT.Exp).then_inc(t_e, 1)

        def p2_act_u(eng, t):
            eng.wait_ge(t_UT, t + 2)
            eng.activation(usT[0][:], bank[5][:].rearrange("p (c q) -> p c q", q=P), ACT.Copy).then_inc(t_uh, 1)

        def p2_act_store(eng, t):
            eng.wait_ge(t_y, 4 * t + 8)
            eng.dma_start(out_rows[bass.ds(t * P, P), :], yo[:]).then_inc(t_out, 16)

        def p2_act(eng):
            for n, (src, dst, w) in enumerate(turned_weights()):
                eng.wait_ge(t_T, n + 1)
                eng.activation(dst[0], bank[n % 2][:, 0:w * len(src)], ACT.Copy).then_inc(t_hi, 1)
            eng.sem_inc(t_out, 16)
            for t in range(3):
                if t == 2:
                    eng.wait_ge(t_x1[0], 16)
                    eng.wait_ge(t_gb[0], 16)
                p2_load(eng, t, t % 2)
            p2_act_ln(eng, 0, 0)
            p2_act_h(eng, 0, 0)
            p2_act_ln(eng, 1, 1)
            p2_act_h(eng, 1, 1)
            p2_act_mid(eng, 0)
            p2_act_u(eng, 0)

            def body(t, slot, ld):
                p2_act_mid(eng, t)
                p2_act_store(eng, t - 1)
                p2_load(eng, t + 2, slot)
                p2_act_ln(eng, t + 1, 1 - slot)
                p2_act_h(eng, t + 1, 1 - slot)
                p2_act_u(eng, t)
            tile_pairs(eng, body)
            t = TILES - 1
            p2_act_mid(eng, t)
            p2_act_store(eng, t - 1)
            p2_act_u(eng, t)
            p2_act_store(eng, t)
            for s in (t_x1[0], t_gb[0]):
                eng.wait_ge(s, 16 * (TILES // 2 + 1))
            eng.wait_ge(t_out, 16 * TILES + 16)

        def p2_dve_ln(eng, t, slot, ld):
            eng.tensor_copy(modcur[:, 1, :, :], modT[1][:, bass.ds(t // QT, 1), :, :].rearrange("p o s k -> p (o s) k")).then_inc(t_mc, 1)
            x1s = tile_slot(x1, t)
            ln_ops(eng, lambda _: x1s, st2, mv2, lnv2, LN2_STEPS, LN2_STEPS * t, t_ln, 1,
                   lambda _: eng.wait_ge(t_x1[slot], 16 * ld), lambda: eng.wait_ge(t_sq, t + 1), lambda _: None)
            if not (isinstance(t, int) and t == 0):
                eng.wait_ge(t_hT, 2 * t)
            eng.tensor_scalar(xn2[:], x1s, lnv2[:, 3, 0:1], lnv2[:, 5, 0:1], ALU.mult, ALU.add).then_inc(t_xn, 1)

        def p2_dve_h(eng, t, slot):
            eng.wait_ge(t_h2h, t + 1)
            eng.tensor_tensor(h2[slot][1][:], hf[:], h2[slot][0][:].bitcast(F32), ALU.subtract).then_inc(t_h2, 1)

        def p2_dve_gate(eng, t):
            base = GATE * t
            cnt = [0]

            def do(ins):
                cnt[0] += 1
                ins.then_inc(t_gate, 1)
                eng.wait_ge(t_gate, base + cnt[0])
            eng.wait_ge(t_G, t + 1)
            do(eng.tensor_copy(logit[:], bank[4][:, 0:E]))
            do(plain(eng.max(top8[:], logit[:])))
            do(plain(eng.max_index(idx8[:], top8[:], logit[:])))
            do(eng.tensor_tensor(gv[:, 0:1], top8[:, 1:2], top8[:, 0:1], ALU.subtract))
            do(eng.tensor_copy(idxf[:], idx8[:]))
            eng.wait_ge(t_e, t + 1)
            do(eng.tensor_scalar(gv[:, 2:3], gv[:, 1:2], 1.0, None, ALU.add))
            do(eng.reciprocal(gv[:, 3:4], gv[:, 2:3]))
            do(eng.tensor_tensor(gv[:, 4:5], gv[:, 3:4], gv[:, 1:2], ALU.mult))
            eng.tensor_scalar(oneh[:, 0, :], iota_t[:], idxf[:, 0:1], gv[:, 3:4], ALU.is_equal, ALU.mult)
            do(eng.tensor_scalar(oneh[:, 1, :], iota_t[:], idxf[:, 1:2], gv[:, 4:5], ALU.is_equal, ALU.mult))
            assert cnt[0] == GATE
            eng.tensor_tensor(wfull[:], oneh[:, 0, :], oneh[:, 1, :], ALU.add).then_inc(t_wf, 1)
            eng.wait_ge(t_wf, t + 1)
            eng.wait_ge(t_U, t + 1)
            eng.wait_ge(t_UT, t + 1)
            eng.tensor_tensor(us[:], bank[2 + 0][:].rearrange("p (e r) -> p e r", r=R), wfull[:, :].unsqueeze(2).broadcast_to([P, E, R]),
                              ALU.mult).then_inc(t_us, 1)

        t_wf = sem("t_wf")

        def p2_dve_u(eng, t):
            eng.wait_ge(t_uh, t + 1)
            eng.tensor_tensor(usT[1][:], bank[5][:].rearrange("p (c q) -> p c q", q=P), usT[0][:].bitcast(F32), ALU.subtract).then_inc(t_ul, 1)

        def p2_dve_y(eng, t, slot, ld):
            eng.wait_ge(t_gb[slot], 16 * ld)
            gbs, x1s = tile_slot(gb, t), tile_slot(x1, t)
            for half in range(2):
                cs = slice(half * 512, (half + 1) * 512)
                eng.wait_ge(t_Y, 2 * t + half + 1)
                if half == 0:
                    eng.wait_ge(t_out, 16 * t + 16)
                eng.tensor_tensor(yo[:, cs], bank[half][:], gbs[:, cs], ALU.mult).then_inc(t_y, 1)
                eng.wait_ge(t_y, 4 * t + 2 * half + 5)
                eng.tensor_tensor(yo[:, cs], yo[:, cs], x1s[:, cs], ALU.add).then_inc(t_y, 1)

        def p2_dve(eng):
            for n, (src, dst, w) in enumerate(turned_weights()):
                eng.wait_ge(t_hi, n + 1)
                eng.tensor_tensor(dst[1], bank[n % 2][:, 0:w * len(src)], dst[0].bitcast(F32), ALU.subtract).then_inc(t_lo, 1)
            eng.wait_ge(t_in, T_IN)
            p2_dve_ln(eng, 0, 0, 1)
            p2_dve_h(eng, 0, 0)
            p2_dve_ln(eng, 1, 1, 1)
            p2_dve_h(eng, 1, 1)
            p2_dve_gate(eng, 0)
            p2_dve_u(eng, 0)

            def body(t, slot, ld):
                p2_dve_gate(eng, t)
                p2_dve_y(eng, t - 1, 1 - slot, ld if slot == 1 else ld - 1)
                p2_dve_ln(eng, t + 1, 1 - slot, ld + (1 if slot == 1 else 0))
                p2_dve_h(eng, t + 1, 1 - slot)
                p2_dve_u(eng, t)
            tile_pairs(eng, body)
            t = TILES - 1
            p2_dve_gate(eng, t)
            p2_dve_y(eng, t - 1, 0, TILES // 2)
            p2_dve_u(eng, t)
            p2_dve_y(eng, t, 1, TILES // 2)

        def p2_pe(eng):
            eng.wait_ge(t_in, T_IN)
            for n, (src, dst, w) in enumerate(turned_weights()):
                if n >= 2:
                    eng.wait_ge(t_lo, n - 1)
                for j, s in enumerate(src):
                    k = s.shape[0]
                    m = eng.transpose(bank[n % 2][:, j * w:(j + 1) * w], s, ident_t[0:k, 0:k])
                m.then_inc(t_T, 1)

            def turn(t):
                eng.wait_ge(t_xn, t + 1)
                if not (isinstance(t, int) and t == 0):
                    eng.wait_ge(t_aff, 2 * t)
                for half in range(2):
                    for k in range(4 * half, 4 * half + 4):
                        m = eng.transpose(bank[6 + half][:, (k % 4) * P:(k % 4 + 1) * P], xn2[:, k * P:(k + 1) * P], ident_t[:])
                    m.then_inc(t_hT, 1)

            def up(t, slot):
                if isinstance(t, int) and t == 0:
                    eng.wait_ge(t_lo, NTURN)
                eng.wait_ge(t_h2, t + 2)
                eng.wait_ge(t_us, t + 1)
                for k in range(KT):
                    m = mm3(eng, bank[4][:, 0:E], sl(h2[slot], lambda h: h[:, k, :]), sl(gT, lambda g: g[:, k, :]), k == 0, k == KT - 1)
                m.then_inc(t_G, 1)
                for k in range(KT):
                    m = mm3(eng, bank[2][:], sl(h2[slot], lambda h: h[:, k, :]), sl(aT, lambda a: a[:, k, :]), k == 0, k == KT - 1)
                m.then_inc(t_U, 1)

            def turn_u(t):
                eng.wait_ge(t_us, t + 2)
                eng.wait_ge(t_ul, t + 1)
                for cc in range(ET):
                    m = eng.transpose(bank[5][:, cc * P:(cc + 1) * P], us[:, 2 * cc:2 * cc + 2, :].rearrange("p e r -> p (e r)"), ident_t[:])
                m.then_inc(t_UT, 1)

            def down(t):
                eng.wait_ge(t_ul, t + 2)
                for half in range(2):
                    eng.wait_ge(t_y, 4 * t + 2 * half + 1)
                    for cc in range(ET):
                        m = mm3(eng, bank[half][:], sl(usT, lambda u: u[:, cc, :]), sl(bT, lambda w: w[:, cc, half * 512:(half + 1) * 512]),
                                cc == 0, cc == ET - 1)
                    m.then_inc(t_Y, 1)

            turn(0)
            up(0, 0)
            turn(1)
            turn_u(0)

            def body(t, slot, ld):
                up(t, slot)
                down(t - 1)
                turn(t + 1)
                turn_u(t)
            tile_pairs(eng, body)
            up(TILES - 1, 1)
            down(TILES - 2)
            turn_u(TILES - 1)
            down(TILES - 1)

        block = top.enter_context(nc.Block())

        @block.sync
        def _(eng):
            p0_sp(eng); phase_end(eng, 0)
            p1_sp(eng)
            for i, s in enumerate(s_stage):
                eng.wait_ge(s, 16 * (5 * GROUPS + 1 - i))
            phase_end(eng, 1)
            p2_sp(eng)

        @block.gpsimd
        def _(eng):
            phase_end(eng, 0)
            p1_pool(eng); phase_end(eng, 1)

        @block.scalar
        def _(eng):
            p0_act(eng); phase_end(eng, 0)
            p1_act(eng); phase_end(eng, 1)
            p2_act(eng)

        @block.vector
        def _(eng):
            p0_dve(eng); phase_end(eng, 0)
            p1_dve(eng); phase_end(eng, 1)
            for s, credit in ((t_h2, 1), (t_us, 1), (t_ul, 1), (t_UT, 1), (t_y, 4)):
                eng.sem_inc(s, credit)
            p2_dve(eng)

        @block.tensor
        def _(eng):
            p0_pe(eng); phase_end(eng, 0)
            p1_pe(eng); phase_end(eng, 1)
            p2_pe(eng)


_INS = {"L0_attn_x": "x", "L0_attn_wq": "wq", "L0_attn_wk": "wk", "L0_attn_wv": "wv", "L0_attn_wo": "wo",
        "L0_ffn_gate_w": "gate_w", "L0_ffn_lora_A": "lora_a", "L0_ffn_lora_B": "lora_b", "L0_c": "c", "L0_wmod": "wmod"}


def kernel(**inputs):
    from concourse import bacc
    from concourse.bass_utils import run_bass_kernel_spmd

    nc = bacc.Bacc("TRN2", target_bir_lowering=False, num_devices=1)
    arrays, args = {}, {}
    given = {_INS[k]: np.ascontiguousarray(v) for k, v in inputs.items()} | constants()
    for name, a in given.items():
        arrays[f"in_{name}"] = a
        args[name] = nc.dram_tensor(f"in_{name}", a.shape, mybir.dt.from_np(a.dtype), kind="ExternalInput").ap()
    args["out"] = nc.dram_tensor("out", (BATCH, SEQ, D), F32, kind="ExternalOutput").ap()
    adaln_block(nc, **args)
    r = run_bass_kernel_spmd(nc, [arrays], core_ids=[0])
    return r.results[0]["out"]
```

```python
from contextlib import ExitStack

import numpy as np

import concourse.bass as bass
from concourse import mybir

F32 = mybir.dt.float32
F32R = mybir.dt.float32r
U32 = mybir.dt.uint32
ALU = mybir.AluOpType
ACT = mybir.ActivationFunctionType

P = 128
BATCH, SEQ, D = 4, 512, 1024
HEADS, KV = 32, 8
GQ = HEADS // KV
HD = 128
WINDOW = 256
KT = D // P
QT = SEQ // P
UNITS = QT * GQ
SCALE = HD ** -0.5
EPS = 1e-5
E, R = 8, 64
ET = E * R // P
TILES = BATCH * QT
FAR = 3.0e38
NEG = -3.0e38
GROUPS = BATCH * KV
NC = 10
FAST_N = 256
LA = 3
LAG = 3
V_TURN = LA + 2


def key_tiles(i):
    return list(range(max(0, i - WINDOW // P), i + 1))


def constants():
    half = HD // 2
    inv = (np.float32(10000.0) ** (-np.arange(half, dtype=np.float32) / np.float32(half))).astype(np.float32)
    ang = inv[:, None] * np.arange(SEQ, dtype=np.float32)[None, :]
    cos, sin = np.cos(ang).astype(np.float32), np.sin(ang).astype(np.float32)
    p, j = np.arange(P)[:, None], np.arange(P)[None, :]
    mask = np.zeros((P, 3 * P), np.float32)
    mask[:, :P][~(j > p)] = NEG
    mask[:, 2 * P:][~(j <= p)] = NEG
    return {
        "cos": np.concatenate([cos, cos]),
        "sin": np.concatenate([-sin, sin]),
        "mask": mask,
        "ident": np.eye(P, dtype=np.float32),
        "iota": np.tile(np.arange(E, dtype=np.float32), (P, 1)),
    }


def adaln_block(nc, x, wq, wk, wv, wo, gate_w, lora_a, lora_b, c, wmod, cos, sin, mask, ident, iota, out):
    x_rows = x.rearrange("b s d -> (b s) d")
    out_rows = out.rearrange("b s d -> (b s) d")
    mod_d = nc.dram_tensor("mod_scratch", (6 * BATCH, D), F32, kind="Internal").ap()
    x1_d = nc.dram_tensor("x1_scratch", (BATCH * SEQ, D), F32, kind="Internal").ap()

    with ExitStack() as top:
        def sb(stack, name, shape, dt=F32):
            return stack.enter_context(nc.sbuf_tensor(name, shape, dt))

        def sem(name):
            return top.enter_context(nc.semaphore(name))

        bank = [top.enter_context(nc.psum_tensor(f"bank{i}", [P, 512], F32)) for i in range(8)]
        ident_t = sb(top, "ident_t", [P, P])
        modT = [sb(top, f"modT{l}", [P, BATCH, 2, KT]) for l in range(2)]
        modcur = sb(top, "modcur", [P, 1, 2, KT])
        barrier = sem("barrier")

        def plain(ins):
            return ins.wait_op(barrier, 5, "sem-ge")

        def phase_end(eng, k):
            eng.drain().then_inc(barrier, 1)
            eng.wait_ge(barrier, 5 * (k + 1))

        p0 = ExitStack()
        wm = [sb(p0, f"wm{i}", [P, KT, 512]) for i in range(2)]
        c_rows = sb(p0, "c_rows", [BATCH, D])
        c_sig = sb(p0, "c_sig", [BATCH, D])
        cT = sb(p0, "cT", [P, KT, BATCH])
        mrow = [sb(p0, f"mrow{i}", [BATCH, 512]) for i in range(2)]
        mabs = sb(p0, "mabs", [BATCH, 512])
        msgn = sb(p0, "msgn", [BATCH, 512])
        p0.close()
        NM = 6 * D // 512
        s_wm = [sem(f"s_wm{i}") for i in range(2)]
        s_c0 = sem("s_c0"); s_id = sem("s_id")
        s_sig = sem("s_sig"); s_v0 = sem("s_v0"); s_ct = sem("s_ct"); s_ctc = sem("s_ctc")
        s_mm0 = sem("s_mm0"); s_mr = sem("s_mr"); s_mt = sem("s_mt"); s_mc = sem("s_mc"); s_md = [sem("s_md0"), sem("s_md1")]

        def is_gate(j):
            return (j // 2) % 3 == 2

        def p0_sp(eng):
            eng.dma_start(ident_t[:], ident).then_inc(s_id, 16)
            eng.dma_start(c_rows[:], c).then_inc(s_c0, 16)
            for j in range(NM):
                if j >= 2:
                    eng.wait_ge(s_mm0, j - 1)
                eng.dma_start(wm[j % 2][:], wmod[:, j * 512:(j + 1) * 512].rearrange("(k p) n -> p k n", p=P)).then_inc(s_wm[j % 2], 16)

        def p0_act(eng):
            eng.wait_ge(s_c0, 16)
            eng.activation(c_sig[:], c_rows[:], ACT.Exp, scale=-1.0).then_inc(s_sig, 1)
            gates = 0
            for j in range(NM):
                eng.wait_ge(s_mm0, j + 1)
                if not is_gate(j):
                    if j >= 2 and not is_gate(j - 2):
                        eng.wait_ge(s_mt, sum(not is_gate(q) for q in range(j - 1)))
                    if j >= 2 and is_gate(j - 2):
                        eng.wait_ge(s_md[j % 2], 16 * sum(is_gate(q) for q in range(j % 2, j - 1, 2)))
                    eng.activation(mrow[j % 2][:], bank[j % 2][0:BATCH, :], ACT.Copy).then_inc(s_mr, 1)
                else:
                    eng.wait_ge(s_v0, v0_done[j])
                    q = j // 2 * BATCH
                    eng.dma_start(mod_d[q:q + BATCH, (j % 2) * 512:(j % 2 + 1) * 512], mrow[j % 2][:]).then_inc(s_md[j % 2], 16)
            for i in range(2):
                eng.wait_ge(s_md[i], 16 * sum(is_gate(q) for q in range(i, NM, 2)))

        v0_done, at = {}, 3
        for j in range(NM):
            at += 6 if is_gate(j) else 1
            v0_done[j] = at

        def p0_dve(eng):
            eng.wait_ge(s_sig, 1)
            eng.tensor_scalar(c_sig[:], c_sig[:], 1.0, None, ALU.add).then_inc(s_v0, 1)
            eng.wait_ge(s_v0, 1)
            eng.reciprocal(c_sig[:], c_sig[:]).then_inc(s_v0, 1)
            eng.wait_ge(s_v0, 2)
            eng.tensor_tensor(c_rows[:], c_rows[:], c_sig[:], ALU.mult).then_inc(s_v0, 1)
            eng.wait_ge(s_ct, 1)
            eng.tensor_copy(cT[:], bank[2][:, 0:KT * BATCH].rearrange("p (k b) -> p k b", b=BATCH)).then_inc(s_ctc, 1)
            turned = 0
            for j in range(NM):
                part, half = divmod(j, 2)
                if is_gate(j):
                    eng.wait_ge(s_mm0, j + 1)
                    if j >= 2 and not is_gate(j - 2):
                        eng.wait_ge(s_mt, turned)
                    v = v0_done[j] - 6
                    acc = bank[j % 2][0:BATCH, :]
                    steps = [
                        lambda: eng.tensor_scalar(mabs[:], acc, -1.0, None, ALU.mult),
                        lambda: eng.tensor_tensor(mabs[:], mabs[:], acc, ALU.max),
                        lambda: eng.tensor_scalar(mabs[:], mabs[:], 0.25, None, ALU.max),
                        lambda: eng.tensor_scalar(msgn[:], acc, 0.0, 2.0, ALU.is_ge, ALU.mult),
                        lambda: eng.tensor_scalar(msgn[:], msgn[:], -1.0, None, ALU.add),
                        lambda: eng.tensor_tensor(mrow[j % 2][:], msgn[:], mabs[:], ALU.mult),
                    ]
                    for n, step in enumerate(steps):
                        eng.wait_ge(s_v0, v + n)
                        step().then_inc(s_v0, 1)
                else:
                    turned += 1
                    eng.wait_ge(s_mt, turned)
                    src = bank[2 + turned % 2][:, 0:4 * BATCH].rearrange("p (k b) -> p b k", b=BATCH)
                    dst = modT[part // 3][:, :, part % 3, half * 4:half * 4 + 4]
                    eng.tensor_scalar(dst, src, float(part % 3), None, ALU.add).then_inc(s_v0, 1)
            eng.wait_ge(s_v0, v0_done[NM - 1])

        def p0_pe(eng):
            eng.wait_ge(s_id, 16)
            eng.wait_ge(s_v0, 3)
            for k in range(KT):
                m = eng.transpose(bank[2][:, k * BATCH:(k + 1) * BATCH], c_rows[:, k * P:(k + 1) * P], ident_t[0:BATCH, 0:BATCH])
            m.then_inc(s_ct, 1)
            eng.wait_ge(s_ctc, 1)
            turned = 0

            def turn(j):
                nonlocal turned
                if is_gate(j):
                    return
                turned += 1
                eng.wait_ge(s_mr, turned)
                if turned >= 3:
                    prev = [q for q in range(NM) if not is_gate(q)][turned - 3]
                    eng.wait_ge(s_v0, v0_done[prev])
                for k in range(4):
                    m = eng.transpose(bank[2 + turned % 2][:, k * BATCH:(k + 1) * BATCH], mrow[j % 2][:, k * P:(k + 1) * P],
                                      ident_t[0:BATCH, 0:BATCH])
                m.then_inc(s_mt, 1)

            for j in range(NM):
                eng.wait_ge(s_wm[j % 2], 16 * (j // 2 + 1))
                if j >= 2:
                    if is_gate(j - 2):
                        eng.wait_ge(s_v0, v0_done[j - 2])
                    else:
                        eng.wait_ge(s_mr, sum(not is_gate(q) for q in range(j - 1)))
                for k in range(KT):
                    m = eng.matmul(bank[j % 2][0:BATCH, :], cT[:, k, :], wm[j % 2][:, k, :], start=k == 0, stop=k == KT - 1)
                m.then_inc(s_mm0, 1)
                if j:
                    turn(j - 1)
            turn(NM - 1)

        p1 = ExitStack()

        def sl(pair, f):
            return tuple(f(t) for t in pair)

        def split_pair(stack, name, shape):
            return sb(stack, name + "_hi", shape, F32R), sb(stack, name + "_lo", shape, F32R)

        hT = split_pair(p1, "hT", [P, KT, SEQ])
        acc = sb(p1, "acc", [P, QT, D])
        w_q = split_pair(p1, "w_q", [P, KT, GQ * HD])
        w_k = split_pair(p1, "w_k", [P, KT, HD])
        w_v = split_pair(p1, "w_v", [P, KT, HD])
        w_o = split_pair(p1, "w_o", [P, GQ, D])
        stage = [sb(p1, f"stage{i}", [P, 1024]) for i in range(2)]
        qo = split_pair(p1, "qo", [P, GQ, SEQ])
        kt_ = split_pair(p1, "kt_", [P, SEQ])
        v_ = split_pair(p1, "v_", [P, QT, HD])
        swapped = [sb(p1, f"swapped{i}", [P, SEQ]) for i in range(2)]
        rotated = [sb(p1, f"rotated{i}", [P, SEQ]) for i in range(2)]
        prob = sb(p1, "prob", [P, GQ, 3 * P])
        cos_t = sb(p1, "cos_t", [P, SEQ])
        sin_t = sb(p1, "sin_t", [P, SEQ])
        mask_t = sb(p1, "mask_t", [P, 3 * P])
        nbias = sb(p1, "nbias", [P, UNITS])
        rowsum = sb(p1, "rowsum", [P, UNITS])
        rrow = sb(p1, "rrow", [P, UNITS])
        stats = sb(p1, "stats", [P, QT, 2, 6])
        mv = sb(p1, "mv", [P, QT, 2])
        lnv = sb(p1, "lnv", [P, 6, QT])
        with ExitStack() as a:
            pT = [split_pair(a, f"pT{i}", [P, 3, GQ * P]) for i in range(2)]
        with ExitStack() as a:
            xb = sb(a, "xb", [P, QT, D])
            ga_t = sb(a, "ga_t", [P, D])
        p1.close()

        s_cst = sem("s_cst")
        s_stage = [sem("s_stage0"), sem("s_stage1")]
        s_split = sem("s_split")
        s_proj = sem("s_proj")
        s_wo = sem("s_wo")
        s_act = sem("s_act")
        s_dve = sem("s_dve")
        s_swp = sem("s_swp"); s_rs = sem("s_rs"); s_ra = sem("s_ra"); s_rh = sem("s_rh")
        s_qk = sem("s_qk")
        s_vt = sem("s_vt"); s_vh = sem("s_vh"); s_v = sem("s_v")
        s_S = sem("s_S"); s_msk = sem("s_msk"); s_exp = sem("s_exp"); s_rl = sem("s_rl"); s_nrm = [sem(f"s_nrm{h}") for h in range(GQ)]
        s_T = sem("s_T"); s_pth = sem("s_pth"); s_ptl = sem("s_ptl"); s_pv = sem("s_pv"); s_oh = sem("s_oh"); s_ol = sem("s_ol")
        s_xb = [sem(f"s_xb{t}") for t in range(QT)]
        s_ga = sem("s_ga"); s_x1 = sem("s_x1")
        s_ln = sem("s_ln"); s_sq = sem("s_sq"); s_xn = sem("s_xn"); s_lnT = sem("s_lnT"); s_lna = sem("s_lna"); s_lnh = sem("s_lnh"); s_h = sem("s_h")
        s_fin = sem("s_fin"); s_acc0 = sem("s_acc0"); s_mc1 = sem("s_mc1")

        LN_STEPS = 3 * QT + 8
        s_wor = sem("s_wor")

        def bank_free(eng, n, name):
            before = {"wo1": 1, "Q1": 1, "Q2": 2, "Q3": 3, "V": 4}
            if name in before:
                eng.wait_ge(s_rs, 5 * n + before[name])

        def chunk_source(j, g):
            if j == 0 or j == 5:
                w = wv if j == 0 else wk
                return w[:, bass.ds(g * HD, HD)].rearrange("(k p) n -> p k n", p=P), "p (k n) -> p k n", dict(n=HD)
            if j <= 4:
                k = 2 * (j - 1)
                return wq[k * P:(k + 2) * P, bass.ds(g * GQ * HD, GQ * HD)].rearrange("(k p) n -> p k n", p=P), "p (k n) -> p k n", dict(k=2)
            return wo[bass.ds(g * GQ * HD + (j - 6) * HD, HD), :], None, None

        def load_chunk(eng, slot, j, g):
            src, pat, kw = chunk_source(j, g)
            dst = stage[slot][:]
            if pat:
                dst = dst.rearrange(pat, **kw)
            eng.dma_start(dst, src).then_inc(s_stage[slot], 16)

        def p1_sp(eng):
            for t, src in ((cos_t, cos), (sin_t, sin), (mask_t, mask)):
                eng.dma_start(t[:], src).then_inc(s_cst, 16)
            load_chunk(eng, 0, 5, 0)
            with eng.Fori(0, GROUPS) as n:
                for j in range(NC):
                    eng.wait_ge(s_split, 10 * n + j + 1)
                    load_chunk(eng, (1 + j) % 2, j, (n + 1) % KV if j == 5 else n % KV)

        s_hi = sem("s_hi")

        def chunk(j):
            slot = (1 + j) % 2
            if j == 0:
                dst = sl(w_v, lambda w: w[:])
            elif j <= 4:
                dst = sl(w_q, lambda w: w[:, 2 * (j - 1):2 * j, :])
            elif j == 5:
                dst = sl(w_k, lambda w: w[:])
            else:
                dst = sl(w_o, lambda w: w[:, j - 6, :])
            src = stage[slot][:]
            if len(dst[0].shape) == 3:
                src = src.rearrange("p (k n) -> p k n", n=dst[0].shape[2])
            return slot, dst, src

        def act_chunk(eng, n, j):
            slot, dst, src = chunk(j)
            if j == 0:
                eng.wait_ge(s_proj, 6 * n + 1)
            elif j == 5:
                eng.wait_ge(s_proj, 6 * n + 2)
            elif j == 6:
                eng.wait_ge(s_wo, 8 * n + 1)
            eng.wait_ge(s_stage[slot], 16 * (5 * n + (1 + j) // 2 + 1))
            eng.activation(dst[0], src, ACT.Copy).then_inc(s_hi, 1)

        def pool_chunk(eng, n, j):
            slot, dst, src = chunk(j)
            eng.wait_ge(s_hi, 10 * n + j + 2)
            eng.tensor_tensor(dst[1], src, dst[0].bitcast(F32), ALU.subtract).then_inc(s_split, 1)

        def first_chunk(eng, pool):
            slot, dst, src = chunk(5)
            if pool:
                eng.wait_ge(s_hi, 1)
                eng.tensor_tensor(dst[1], src, dst[0].bitcast(F32), ALU.subtract).then_inc(s_split, 1)
            else:
                eng.wait_ge(s_stage[slot], 16)
                eng.activation(dst[0], src, ACT.Copy).then_inc(s_hi, 1)

        def p1_pool(eng):
            eng.sem_inc(s_split, 1)
            first_chunk(eng, True)
            with eng.Fori(0, GROUPS) as n:
                for j in range(NC):
                    pool_chunk(eng, n, j)

        def mm3(eng, o, st, mv_, start, stop):
            eng.matmul(o, st[0], mv_[0], start=start, stop=False)
            eng.matmul(o, st[0], mv_[1], start=False, stop=False)
            return eng.matmul(o, st[1], mv_[0], start=False, stop=stop)

        def pe_project(eng, n, name, w, cols, bk, waits):
            bank_free(eng, n, name)
            for k in range(KT):
                if k in waits:
                    eng.wait_ge(*waits[k])
                m = mm3(eng, bank[bk][:], sl(w, lambda t: t[:, k, cols]), sl(hT, lambda t: t[:, k, :]), k == 0, k == KT - 1)
            m.then_inc(s_proj, 1)

        def pe_wo(eng, n, half, first_of_bank):
            t, c = divmod(half, 2)
            if half == 0:
                eng.wait_ge(s_ol, QT * n + QT)
            if half >= 2:
                eng.wait_ge(s_wor, 8 * n + half)
            elif first_of_bank is not None:
                first_of_bank(half)
            for h in range(GQ):
                m = mm3(eng, bank[1 - half % 2][:], sl(qo, lambda q: q[:, h, t * P:(t + 1) * P]),
                        sl(w_o, lambda w: w[:, h, c * 512:(c + 1) * 512]), h == 0, h == GQ - 1)
            m.then_inc(s_wo, 1)

        SBANK = [bank[2], bank[3], bank[4], bank[0]]
        OBANK = [bank[7], bank[1]]

        def pe_scores(eng, n, u):
            i, h = divmod(u, GQ)
            kts = key_tiles(i)
            if i == 0:
                eng.wait_ge(s_qk, 5 * n + 2 + h)
            if u >= 4:
                eng.wait_ge(s_msk, UNITS * n + u - 3)
            cols = max(P * len(kts), FAST_N)
            mm3(eng, SBANK[u % 4][:, 0:cols], sl(qo, lambda q: q[:, h, i * P:(i + 1) * P]),
                sl(kt_, lambda k: k[:, kts[0] * P:kts[0] * P + cols]), True, True).then_inc(s_S, 1)

        def pe_turn(eng, n, u):
            eng.wait_ge(s_nrm[u % GQ], QT * n + u // GQ + 1)
            if u >= 2:
                eng.wait_ge(s_ptl, UNITS * n + u - 1)
            for b in range(len(key_tiles(u // GQ))):
                m = eng.transpose(bank[5 + u % 2][:, b * P:(b + 1) * P], prob[:, u % GQ, b * P:(b + 1) * P], ident_t[:])
            m.then_inc(s_T, 1)

        def pe_values(eng, n, i):
            eng.wait_ge(s_ptl, UNITS * n + GQ * (i + 1))
            if i == 0:
                eng.wait_ge(s_v, n + 2)
            elif i >= 2:
                eng.wait_ge(s_ol, QT * n + i - 1)
            kts = key_tiles(i)
            for b, kt in enumerate(kts):
                m = mm3(eng, OBANK[i % 2][:], sl(v_, lambda v: v[:, kt, :]), sl(pT[i % 2], lambda p: p[:, b, :]), b == 0, b == len(kts) - 1)
            m.then_inc(s_pv, 1)

        def pe_attention(eng, n):
            for u in range(UNITS):
                if u + LA < UNITS:
                    pe_scores(eng, n, u + LA)
                pe_turn(eng, n, u)
                if u == 1:
                    eng.wait_ge(s_act, 7 * n + 6)
                    for t in range(QT):
                        m = eng.transpose(bank[7][:, t * P:(t + 1) * P], swapped[1][:, t * P:(t + 1) * P], ident_t[:])
                    m.then_inc(s_vt, 1)
                if u % GQ == 1 and GQ < u < UNITS - GQ:
                    pe_values(eng, n, u // GQ - 1)
            for i in (QT - 2, QT - 1):
                pe_values(eng, n, i)

        def pe_k(eng, n, b=None):
            waits = {0: (s_split, 10 * n + 2)}
            if b is None:
                pe_project(eng, n, "K", w_k, slice(0, HD), 0, waits)
                return
            eng.wait_ge(s_wor, 8 * n + 1)
            eng.wait_ge(*waits[0])
            for k in range(KT):
                eng.wait_ge(s_h, KT * b + k + 1)
                m = mm3(eng, bank[0][:], sl(w_k, lambda t: t[:, k, :]), sl(hT, lambda t: t[:, k, :]), k == 0, k == KT - 1)
            m.then_inc(s_proj, 1)

        def pe_qv(eng, n):
            for h in range(GQ):
                waits = {2 * q: (s_split, 10 * n + 4 + q) for q in range(4)} if h == 0 else {}
                pe_project(eng, n, f"Q{h}", w_q, slice(h * HD, (h + 1) * HD), 1 - h % 2, waits)
            for u in range(LA):
                pe_scores(eng, n, u)
            pe_project(eng, n, "V", w_v, slice(0, HD), 1, {})

        def pe_ln_turn(eng, b1, m_):
            for k in range(KT):
                if k == 0:
                    eng.wait_ge(s_xn, QT * b1 + QT)
                if k >= 2:
                    eng.wait_ge(s_lna, KT * b1 + k - 1)
                for t in range(QT):
                    m = eng.transpose(bank[2 + k % 2][:, t * P:(t + 1) * P], xb[:, t, k * P:(k + 1) * P], ident_t[:])
                m.then_inc(s_lnT, 1)

        def p1_pe(eng):
            eng.sem_inc(s_proj, 1)
            eng.sem_inc(s_wo, 1)
            pe_ln_turn(eng, 0, None)
            with eng.Fori(0, BATCH) as b:
                pe_k(eng, KV * b, b)
                pe_qv(eng, KV * b)
                pe_attention(eng, KV * b)
                with eng.Fori(1, KV) as g:
                    n = b * KV + g
                    pe_k(eng, n)
                    for half in range(8):
                        pe_wo(eng, n - 1, half, lambda hf: bank_free(eng, n, f"wo{hf}"))
                    eng.wait_ge(s_wor, 8 * n + 1)
                    pe_qv(eng, n)
                    pe_attention(eng, n)
                n = b * KV + (KV - 1)
                eng.wait_ge(s_split, 10 * n + 12)
                for half in range(6):
                    pe_wo(eng, n, half, None)
                pe_ln_turn(eng, b + 1, None)
                for half in range(6, 8):
                    pe_wo(eng, n, half, None)

        ACT_NORM = ()
        OUT_STEP = {GQ * i + GQ + 1 + LAG: i for i in range(QT - 2)}

        def act_rope(eng, n, r):
            slot = r % 2
            eng.wait_ge(s_dve, 5 * n + r + 1)
            if r >= 2:
                eng.wait_ge(s_qk, 5 * n + r - 1)
            half = HD // 2
            bk = bank[0 if r % 2 == 0 else 1]
            eng.activation(swapped[slot][0:half, :], bk[half:HD, :], ACT.Copy)
            eng.activation(swapped[slot][half:HD, :], bk[0:half, :], ACT.Copy).then_inc(s_act, 1)
            if r:
                act_chunk(eng, n, 5 + r)
            dst = kt_[0][:] if r == 0 else qo[0][:, r - 1, :]
            eng.wait_ge(s_ra, 5 * n + r + 1)
            eng.activation(dst, rotated[slot][:], ACT.Copy).then_inc(s_rh, 1)

        def act_project(eng, n):
            for j in (0, 1):
                act_chunk(eng, n, j)
            act_rope(eng, n, 0)
            for j in (2, 3, 4, 5):
                act_chunk(eng, n, j)
            for r in range(1, 1 + GQ):
                act_rope(eng, n, r)

        def act_attention(eng, n, first):
            for s in range(UNITS + LAG):
                if s == LA:
                    eng.wait_ge(s_proj, 6 * n + 7)
                    eng.wait_ge(s_qk, 5 * n + 4)
                    eng.activation(swapped[1][:], bank[1][:], ACT.Copy).then_inc(s_act, 1)
                if s == V_TURN:
                    eng.wait_ge(s_vt, n + 1)
                    eng.activation(v_[0][:], bank[7][:].rearrange("p (t d) -> p t d", d=HD), ACT.Copy).then_inc(s_act, 1)
                u = s - LAG
                if 0 <= u < UNITS:
                    i, h = divmod(u, GQ)
                    eng.wait_ge(s_T, UNITS * n + u + 1)
                    if h == 0 and i >= 2:
                        eng.wait_ge(s_pv, QT * n + i - 1)
                    if u == 0 and first is not None:
                        eng.wait_ge(s_x1, 16 * QT * first + 16)
                    nk = len(key_tiles(i))
                    eng.activation(pT[i % 2][0][:, 0:nk, h * P:(h + 1) * P],
                                   bank[5 + u % 2][:, 0:nk * P].rearrange("p (b q) -> p b q", q=P), ACT.Copy).then_inc(s_pth, 1)
                if s < UNITS:
                    w = P * len(key_tiles(s // GQ))
                    tile = prob[:, s % GQ, 0:w]
                    eng.wait_ge(s_msk, UNITS * n + s + 1)
                    eng.activation(tile, tile, ACT.Exp, bias=nbias[:, s:s + 1], scale=-1.0,
                                   accum_out=rowsum[:, s:s + 1]).then_inc(s_exp, 1)
                if 1 <= s < UNITS + 1 and (s - 1) % GQ in ACT_NORM:
                    tile = prob[:, (s - 1) % GQ, 0:P * len(key_tiles((s - 1) // GQ))]
                    eng.wait_ge(s_rl, UNITS * n + s)
                    eng.activation(tile, tile, ACT.Copy, scale=rrow[:, s - 1:s]).then_inc(s_nrm[(s - 1) % GQ], 1)
                if s in OUT_STEP:
                    act_outputs(eng, n, OUT_STEP[s])
            for i in (QT - 2, QT - 1):
                act_outputs(eng, n, i)

        def act_outputs(eng, n, i):
            eng.wait_ge(s_pv, QT * n + i + 1)
            eng.activation(qo[0][:, :, i * P:(i + 1) * P], OBANK[i % 2][:].rearrange("p (h q) -> p h q", q=P), ACT.Copy).then_inc(s_oh, 1)

        def act_load_x(eng, b, tiles):
            for t in tiles:
                eng.dma_start(xb[:, t, :], x_rows[bass.ds(b * SEQ + t * P, P), :]).then_inc(s_xb[t], 16)

        def act_ln(eng, b1):
            eng.wait_ge(s_ln, LN_STEPS * b1 + LN_VAR)
            eng.activation(lnv[:, 1, :], lnv[:, 0, :], ACT.Sqrt).then_inc(s_sq, 1)
            for k in range(KT):
                eng.wait_ge(s_lnT, KT * b1 + k + 1)
                if k == 0:
                    eng.wait_ge(s_mc1, b1 + 1)
                if k >= 2:
                    eng.wait_ge(s_h, KT * b1 + k - 1)
                eng.activation(rotated[k % 2][:], bank[2 + k % 2][:], ACT.Identity, bias=modcur[:, 0, 0, k:k + 1],
                               scale=modcur[:, 0, 1, k:k + 1]).then_inc(s_lna, 1)
                eng.wait_ge(s_lna, KT * b1 + k + 1)
                eng.activation(hT[0][:, k, :], rotated[k % 2][:], ACT.Copy).then_inc(s_lnh, 1)

        def p1_act(eng):
            eng.sem_inc(s_x1, 16)
            act_load_x(eng, 0, range(QT))
            first_chunk(eng, False)
            act_ln(eng, 0)
            with eng.Fori(0, BATCH) as b:
                act_project(eng, KV * b)
                act_attention(eng, KV * b, b)
                with eng.Fori(1, KV) as g:
                    n = b * KV + g
                    act_project(eng, n)
                    act_attention(eng, n, None)
                n = b * KV + (KV - 1)
                act_load_x(eng, (b + 1) % BATCH, range(QT))
                eng.dma_start(ga_t[:], mod_d[bass.ds(2 * BATCH + b, 1), :].broadcast_to([P, D])).then_inc(s_ga, 16)
                act_ln(eng, b + 1)
                act_load_x(eng, b, range(QT))
                for t in range(QT):
                    eng.wait_ge(s_fin, 2 * QT * b + 2 * t + 2)
                    eng.dma_start(x1_d[bass.ds(b * SEQ + t * P, P), :], xb[:, t, :]).then_inc(s_x1, 16)
            eng.wait_ge(s_x1, 16 * TILES + 16)

        LN_VAR = 3 * QT + 1

        def dve_rope(eng, n, r):
            slot = r % 2
            bk = bank[0 if r % 2 == 0 else 1]
            eng.wait_ge(s_proj, 6 * n + 2 + r)
            eng.tensor_tensor(rotated[slot][:], bk[:], cos_t[:], ALU.mult).then_inc(s_dve, 1)
            eng.wait_ge(s_act, 7 * n + r + 1)
            eng.tensor_tensor(swapped[slot][:], swapped[slot][:], sin_t[:], ALU.mult).then_inc(s_rs, 1)
            eng.wait_ge(s_rs, 5 * n + r + 1)
            eng.wait_ge(s_dve, 5 * n + r + 1)
            eng.tensor_tensor(rotated[slot][:], rotated[slot][:], swapped[slot][:], ALU.add).then_inc(s_ra, 1)
            eng.wait_ge(s_rh, 5 * n + r + 1)
            eng.wait_ge(s_ra, 5 * n + r + 1)
            hi, lo = (kt_[0][:], kt_[1][:]) if r == 0 else (qo[0][:, r - 1, :], qo[1][:, r - 1, :])
            eng.tensor_tensor(lo, rotated[slot][:], hi.bitcast(F32), ALU.subtract).then_inc(s_qk, 1)

        def dve_wo(eng, n, half):
            t, cc = divmod(half, 2)
            eng.wait_ge(s_wo, 8 * n + half + 2)
            a = acc[:, t, cc * 512:(cc + 1) * 512]
            eng.tensor_tensor(a, bank[1 - half % 2][:], a, ALU.add).then_inc(s_wor, 1)

        def dve_outputs(eng, n, i):
            eng.wait_ge(s_oh, QT * n + i + 1)
            o = OBANK[i % 2][:].rearrange("p (h q) -> p h q", q=P)
            eng.tensor_tensor(qo[1][:, :, i * P:(i + 1) * P], o, qo[0][:, :, i * P:(i + 1) * P].bitcast(F32),
                              ALU.subtract).then_inc(s_ol, 1)

        def dve_attention(eng, n):
            for s in range(UNITS + LAG):
                if s == V_TURN:
                    eng.wait_ge(s_act, 7 * n + 7)
                    eng.tensor_tensor(v_[1][:], bank[7][:].rearrange("p (t d) -> p t d", d=HD), v_[0][:].bitcast(F32),
                                      ALU.subtract).then_inc(s_v, 1)
                if s < UNITS:
                    w = P * len(key_tiles(s // GQ))
                    eng.wait_ge(s_S, UNITS * n + s + 1)
                    if s >= GQ:
                        eng.wait_ge(s_T, UNITS * n + s - GQ + 1)
                    plain(eng.tensor_tensor_reduce(prob[:, s % GQ, 0:w], SBANK[s % 4][:, 0:w], mask_t[:, 3 * P - w:3 * P], -SCALE, FAR,
                                             ALU.add, ALU.min, nbias[:, s:s + 1])).then_inc(s_msk, 1)
                u = s - LAG
                if 0 <= u < UNITS:
                    i, h = divmod(u, GQ)
                    nk = len(key_tiles(i))
                    eng.wait_ge(s_pth, UNITS * n + u + 1)
                    hi, lo = (p[:, 0:nk, h * P:(h + 1) * P] for p in pT[i % 2])
                    eng.tensor_tensor(lo, bank[5 + u % 2][:, 0:nk * P].rearrange("p (b q) -> p b q", q=P), hi.bitcast(F32),
                                      ALU.subtract).then_inc(s_ptl, 1)
                if 1 <= s < UNITS + 1:
                    eng.wait_ge(s_exp, UNITS * n + s)
                    eng.reciprocal(rrow[:, s - 1:s], rowsum[:, s - 1:s]).then_inc(s_rl, 1)
                    if (s - 1) % 4 not in ACT_NORM:
                        eng.wait_ge(s_rl, UNITS * n + s)
                        tile = prob[:, (s - 1) % GQ, 0:P * len(key_tiles((s - 1) // GQ))]
                        eng.tensor_scalar(tile, tile, rrow[:, s - 1:s], None, ALU.mult).then_inc(s_nrm[(s - 1) % 4], 1)
                if s in OUT_STEP:
                    dve_outputs(eng, n, OUT_STEP[s])
            for i in (QT - 2, QT - 1):
                dve_outputs(eng, n, i)

        def ln_ops(eng, xt, st, mv_, lv, steps, base, semaphore, ntile, wait_x, wait_sq, fill):
            cnt = [0]

            def do(ins):
                cnt[0] += 1
                ins.then_inc(semaphore, 1)

            def after():
                eng.wait_ge(semaphore, base + cnt[0])

            for t in range(ntile):
                wait_x(t)
                do(plain(eng.bn_stats(st[:, t, 0, :], xt(t)[:, 0:512])))
                do(eng.bn_stats(st[:, t, 1, :], xt(t)[:, 512:1024]))
                after()
                do(plain(eng.bn_aggr(mv_[:, t, :], st[:, t, :, :].rearrange("p a s -> p (a s)"))))
                fill(t)
            after()
            do(eng.tensor_scalar(lv[:, 0, :], mv_[:, :, 1], EPS, None, ALU.add))
            wait_sq()
            do(eng.reciprocal(lv[:, 1, :], lv[:, 1, :])); after()
            do(eng.tensor_tensor(lv[:, 2, :], lv[:, 1, :], lv[:, 1, :], ALU.mult)); after()
            do(eng.tensor_tensor(lv[:, 2, :], lv[:, 2, :], lv[:, 0, :], ALU.mult)); after()
            do(eng.tensor_scalar(lv[:, 2, :], lv[:, 2, :], -0.5, 1.5, ALU.mult, ALU.add)); after()
            do(eng.tensor_tensor(lv[:, 3, :], lv[:, 2, :], lv[:, 1, :], ALU.mult)); after()
            do(eng.tensor_scalar(lv[:, 4, :], mv_[:, :, 0], -1.0, None, ALU.mult)); after()
            do(eng.tensor_tensor(lv[:, 5, :], lv[:, 4, :], lv[:, 3, :], ALU.mult)); after()
            assert cnt[0] == steps, cnt

        def dve_ln(eng, b1, b, xloads, fill, fill2):
            eng.tensor_copy(modcur[:, 0, :, :], modT[0][:, bass.ds(b, 1), :, :].rearrange("p o s k -> p (o s) k")).then_inc(s_mc1, 1)
            ln_ops(eng, lambda t: xb[:, t, :], stats, mv, lnv, LN_STEPS, LN_STEPS * b1, s_ln, QT,
                   lambda t: eng.wait_ge(s_xb[t], 16 * xloads), lambda: eng.wait_ge(s_sq, b1 + 1), fill)
            for t in range(QT):
                eng.tensor_scalar(xb[:, t, :], xb[:, t, :], lnv[:, 3, t:t + 1], lnv[:, 5, t:t + 1], ALU.mult, ALU.add).then_inc(s_xn, 1)
            fill2()
            for k in range(KT):
                eng.wait_ge(s_lnh, KT * b1 + k + 1)
                eng.tensor_tensor(hT[1][:, k, :], rotated[k % 2][:], hT[0][:, k, :].bitcast(F32), ALU.subtract).then_inc(s_h, 1)

        def p1_dve(eng):
            eng.sem_inc(s_v, 1)
            eng.sem_inc(s_wor, 1)
            eng.memset(acc[:], 0.0).then_inc(s_acc0, 1)
            eng.wait_ge(s_cst, 48)
            dve_ln(eng, 0, 0, 1, lambda t: None, lambda: None)
            with eng.Fori(0, BATCH) as b:
                for r in range(1 + GQ):
                    dve_rope(eng, KV * b, r)
                dve_attention(eng, KV * b)
                with eng.Fori(1, KV) as g:
                    n = b * KV + g
                    dve_rope(eng, n, 0)
                    eng.wait_ge(s_acc0, b + 1)
                    for half in range(8):
                        dve_wo(eng, n - 1, half)
                    for r in range(1, 1 + GQ):
                        dve_rope(eng, n, r)
                    dve_attention(eng, n)
                n = b * KV + (KV - 1)

                def fill2():
                    dve_wo(eng, n, 4)
                    dve_wo(eng, n, 5)
                dve_ln(eng, b + 1, (b + 1) % BATCH, 2 * b + 2, lambda t: dve_wo(eng, n, t), fill2)
                dve_wo(eng, n, 6)
                dve_wo(eng, n, 7)
                eng.wait_ge(s_ga, 16 * b + 16)
                eng.wait_ge(s_wor, 8 * n + 9)
                for t in range(QT):
                    eng.tensor_tensor(acc[:, t, :], acc[:, t, :], ga_t[:], ALU.mult).then_inc(s_fin, 1)
                    eng.wait_ge(s_fin, 2 * QT * b + 2 * t + 1)
                    eng.wait_ge(s_xb[t], 16 * (2 * b + 3))
                    eng.tensor_tensor(xb[:, t, :], xb[:, t, :], acc[:, t, :], ALU.add).then_inc(s_fin, 1)
                eng.wait_ge(s_fin, 2 * QT * b + 2 * QT)
                eng.memset(acc[:], 0.0).then_inc(s_acc0, 1)

        p2 = ExitStack()
        SLOTS = 4

        def tile_slot(buf, t):
            return buf[:, bass.ds(t % SLOTS, 1), :].rearrange("p o d -> p (o d)")

        aT = split_pair(p2, "aT", [P, KT, E * R])
        bT = split_pair(p2, "bT", [P, ET, D])
        gT = split_pair(p2, "gT", [P, KT, E])
        h2 = [split_pair(p2, f"h2{i}", [P, KT, P]) for i in range(2)]
        hf = sb(p2, "hf", [P, KT, P])
        x1 = sb(p2, "x1", [P, SLOTS, D])
        xn2 = sb(p2, "xn2", [P, D])
        gb = sb(p2, "gb", [P, SLOTS, D])
        us = sb(p2, "us", [P, E, R])
        usT = split_pair(p2, "usT", [P, ET, P])
        yo = sb(p2, "yo", [P, D])
        mod2 = [sb(p2, f"mod2{i}", [P, 2, KT]) for i in range(2)]
        st2 = sb(p2, "st2", [P, 1, 2, 6])
        mv2 = sb(p2, "mv2", [P, 1, 2])
        lnv2 = sb(p2, "lnv2", [P, 6, 1])
        lgT = sb(p2, "lgT", [E, P])
        logit = sb(p2, "logit", [P, E])
        top8 = sb(p2, "top8", [P, E])
        idx8 = sb(p2, "idx8", [P, E], U32)
        idxf = sb(p2, "idxf", [P, E])
        gv = sb(p2, "gv", [P, 8])
        oneh = sb(p2, "oneh", [P, 2, E])
        wfull = sb(p2, "wfull", [P, E])
        iota_t = sb(p2, "iota_t", [P, E])
        a_in = sb(p2, "a_in", [P, ET, D])
        b_in = sb(p2, "b_in", [P, KT, E, R])
        g_in = sb(p2, "g_in", [E, D])
        p2.close()

        t_in = sem("t_in"); t_T = sem("t_T"); t_hi = sem("t_hi"); t_lo = sem("t_lo")
        t_x1 = [sem("t_x10"), sem("t_x11")]; t_gb = [sem("t_gb0"), sem("t_gb1")]
        t_ln = sem("t_ln"); t_sq = sem("t_sq"); t_xn = sem("t_xn"); t_hT = sem("t_hT"); t_aff = sem("t_aff")
        t_h2h = sem("t_h2h"); t_h2 = sem("t_h2"); t_mc = sem("t_mc")
        t_lg = sem("t_lg"); t_GT = sem("t_GT"); t_hfree = sem("t_hfree"); t_ya = sem("t_ya")
        t_U = sem("t_U"); t_G = sem("t_G"); t_gate = sem("t_gate"); t_e = sem("t_e"); t_us = sem("t_us"); t_UT = sem("t_UT")
        t_uh = sem("t_uh"); t_ul = sem("t_ul"); t_Y = sem("t_Y"); t_y = sem("t_y"); t_out = sem("t_out")
        NTURN = KT + 2 * ET + 1
        LN2_STEPS = 3 + 8
        GATE = 9

        def turned_weights():
            for k in range(KT):
                yield [a_in[:, cc, k * P:(k + 1) * P] for cc in range(ET)], sl(aT, lambda a: a[:, k, :]), P
            for cc in range(ET):
                for half in range(2):
                    yield [b_in[:, 4 * half + j, 2 * cc:2 * cc + 2, :].rearrange("p e r -> p (e r)") for j in range(4)], \
                        sl(bT, lambda w: w[:, cc, half * 512:(half + 1) * 512]), P
            yield [g_in[:, k * P:(k + 1) * P] for k in range(KT)], sl(gT, lambda g: g[:].rearrange("p k e -> p (k e)")), E

        def p2_sp(eng):
            eng.dma_start(a_in[:], lora_a.rearrange("(c e) r d -> (e r) c d", e=2)).then_inc(t_in, 16)
            for e in range(E):
                eng.dma_start(b_in[:, :, e, :], lora_b[e].rearrange("(k p) r -> p k r", p=P)).then_inc(t_in, 16)
            eng.dma_start(g_in[:], gate_w).then_inc(t_in, 16)
            eng.dma_start(iota_t[:], iota).then_inc(t_in, 16)

        def p2_sp_tiles(eng):
            eng.sem_inc(t_out, 16)
            for t in range(3):
                if t == 2:
                    eng.wait_ge(t_x1[0], 16)
                    eng.wait_ge(t_gb[0], 16)
                p2_load(eng, t, t % 2)

            def body(t, slot, ld):
                eng.wait_ge(t_x1[slot], 16 * ld)
                eng.wait_ge(t_gb[slot], 16 * ld)
                p2_load(eng, t + 2, slot)
                p2_store(eng, t - 1)
            tile_pairs(eng, body)
            for t in (TILES - 2, TILES - 1):
                p2_store(eng, t)
            for s in (t_x1[0], t_gb[0]):
                eng.wait_ge(s, 16 * (TILES // 2 + 1))
            eng.wait_ge(t_out, 16 * TILES + 16)

        T_IN = 16 * (3 + E)

        def p2_load(eng, t, slot):
            eng.dma_start(tile_slot(x1, t), x1_d[bass.ds(t % TILES * P, P), :]).then_inc(t_x1[slot], 16)
            eng.dma_start(tile_slot(gb, t), mod_d[bass.ds(5 * BATCH + t % TILES // QT, 1), :].broadcast_to([P, D])).then_inc(t_gb[slot], 16)

        def tile_pairs(eng, body):
            with eng.Fori(0, TILES // 2 - 1) as q:
                for z in range(2):
                    body(2 * q + 1 + z, (1 + z) % 2, q + (1 if z == 0 else 2))

        def p2_act_ln(eng, t, slot):
            eng.wait_ge(t_ln, LN2_STEPS * t + 4)
            eng.activation(lnv2[:, 1, :], lnv2[:, 0, :], ACT.Sqrt).then_inc(t_sq, 1)

        def p2_act_h(eng, t, slot):
            for half in range(2):
                eng.wait_ge(t_hT, 2 * t + half + 1)
                if half == 0:
                    eng.wait_ge(t_mc, t + 1)
                    eng.wait_ge(t_h2, t + 1)
                for k in range(4 * half, 4 * half + 4):
                    ins = eng.activation(hf[:, k, :], bank[6 + half][:, (k % 4) * P:(k % 4 + 1) * P], ACT.Identity,
                                         bias=mod2[slot][:, 0, k:k + 1], scale=mod2[slot][:, 1, k:k + 1])
                ins.then_inc(t_aff, 1)
            eng.wait_ge(t_aff, 2 * t + 2)
            eng.activation(h2[slot][0][:], hf[:], ACT.Copy).then_inc(t_h2h, 1)

        def p2_act_mid(eng, t):
            eng.wait_ge(t_G, t + 1)
            eng.activation(lgT[:], bank[4][0:E, 0:P], ACT.Copy).then_inc(t_lg, 1)
            eng.wait_ge(t_gate, GATE * t + 4)
            eng.activation(gv[:, 1:2], gv[:, 0:1], ACT.Exp).then_inc(t_e, 1)

        def p2_act_u(eng, t):
            eng.wait_ge(t_UT, t + 2)
            eng.activation(usT[0][:], bank[5][:].rearrange("p (c q) -> p c q", q=P), ACT.Copy).then_inc(t_uh, 1)

        def p2_store(eng, t):
            eng.wait_ge(t_ya, 2 * t + 2)
            eng.dma_start(out_rows[bass.ds(t * P, P), :], yo[:]).then_inc(t_out, 16)

        def p2_act(eng):
            for n, (src, dst, w) in enumerate(turned_weights()):
                eng.wait_ge(t_T, n + 1)
                eng.activation(dst[0], bank[n % 2][:, 0:w * len(src)], ACT.Copy).then_inc(t_hi, 1)
            p2_act_ln(eng, 0, 0)
            p2_act_h(eng, 0, 0)
            p2_act_ln(eng, 1, 1)
            p2_act_mid(eng, 0)
            p2_act_h(eng, 1, 1)
            p2_act_u(eng, 0)

            def body(t, slot, ld):
                p2_act_ln(eng, t + 1, 1 - slot)
                p2_act_mid(eng, t)
                p2_act_h(eng, t + 1, 1 - slot)
                p2_act_u(eng, t)
            tile_pairs(eng, body)
            t = TILES - 1
            p2_act_mid(eng, t)
            p2_act_u(eng, t)

        def p2_dve_ln(eng, t, slot, ld):
            eng.tensor_copy(mod2[slot][:], modT[1][:, bass.ds(t // QT, 1), :, :].rearrange("p o s k -> p (o s) k")).then_inc(t_mc, 1)
            x1s = tile_slot(x1, t)
            ln_ops(eng, lambda _: x1s, st2, mv2, lnv2, LN2_STEPS, LN2_STEPS * t, t_ln, 1,
                   lambda _: eng.wait_ge(t_x1[slot], 16 * ld), lambda: eng.wait_ge(t_sq, t + 1), lambda _: None)
            if not (isinstance(t, int) and t == 0):
                eng.wait_ge(t_hT, 2 * t)
            eng.tensor_scalar(xn2[:], x1s, lnv2[:, 3, 0:1], lnv2[:, 5, 0:1], ALU.mult, ALU.add).then_inc(t_xn, 1)

        def p2_pool_h(eng, t, slot):
            eng.wait_ge(t_h2h, t + 1)
            plain(eng.tensor_tensor(h2[slot][1][:], hf[:], h2[slot][0][:].bitcast(F32), ALU.subtract)).then_inc(t_h2, 1)

        def p2_dve_gate(eng, t):
            base = GATE * t
            cnt = [0]

            def do(ins):
                cnt[0] += 1
                ins.then_inc(t_gate, 1)
                eng.wait_ge(t_gate, base + cnt[0])
            eng.wait_ge(t_GT, t + 1)
            do(eng.tensor_copy(logit[:], bank[3][:, 0:E]))
            do(plain(eng.max(top8[:], logit[:])))
            do(plain(eng.max_index(idx8[:], top8[:], logit[:])))
            do(eng.tensor_tensor(gv[:, 0:1], top8[:, 1:2], top8[:, 0:1], ALU.subtract))
            do(eng.tensor_copy(idxf[:], idx8[:]))
            eng.wait_ge(t_e, t + 1)
            do(eng.tensor_scalar(gv[:, 2:3], gv[:, 1:2], 1.0, None, ALU.add))
            do(eng.reciprocal(gv[:, 3:4], gv[:, 2:3]))
            do(eng.tensor_tensor(gv[:, 4:5], gv[:, 3:4], gv[:, 1:2], ALU.mult))
            eng.tensor_scalar(oneh[:, 0, :], iota_t[:], idxf[:, 0:1], gv[:, 3:4], ALU.is_equal, ALU.mult)
            do(eng.tensor_scalar(oneh[:, 1, :], iota_t[:], idxf[:, 1:2], gv[:, 4:5], ALU.is_equal, ALU.mult))
            assert cnt[0] == GATE
            eng.tensor_tensor(wfull[:], oneh[:, 0, :], oneh[:, 1, :], ALU.add).then_inc(t_wf, 1)
            eng.wait_ge(t_wf, t + 1)
            eng.wait_ge(t_U, t + 1)
            eng.wait_ge(t_UT, t + 1)
            eng.tensor_tensor(us[:], bank[2 + 0][:].rearrange("p (e r) -> p e r", r=R), wfull[:, :].unsqueeze(2).broadcast_to([P, E, R]),
                              ALU.mult).then_inc(t_us, 1)

        t_wf = sem("t_wf")

        def p2_dve_u(eng, t):
            eng.wait_ge(t_uh, t + 1)
            eng.tensor_tensor(usT[1][:], bank[5][:].rearrange("p (c q) -> p c q", q=P), usT[0][:].bitcast(F32), ALU.subtract).then_inc(t_ul, 1)

        def p2_dve_y(eng, t, slot, ld):
            eng.wait_ge(t_gb[slot], 16 * ld)
            gbs = tile_slot(gb, t)
            for half in range(2):
                cs = slice(half * 512, (half + 1) * 512)
                eng.wait_ge(t_Y, 2 * t + half + 1)
                if half == 0:
                    eng.wait_ge(t_out, 16 * t + 16)
                eng.tensor_tensor(yo[:, cs], bank[half][:], gbs[:, cs], ALU.mult).then_inc(t_y, 1)

        def p2_pool_y(eng, t, slot, ld):
            eng.wait_ge(t_x1[slot], 16 * ld)
            x1s = tile_slot(x1, t)
            for half in range(2):
                cs = slice(half * 512, (half + 1) * 512)
                eng.wait_ge(t_y, 2 * t + half + 3)
                plain(eng.tensor_tensor(yo[:, cs], yo[:, cs], x1s[:, cs], ALU.add)).then_inc(t_ya, 1)

        def p2_pool(eng):
            p2_pool_h(eng, 0, 0)
            p2_pool_h(eng, 1, 1)

            def body(t, slot, ld):
                p2_pool_h(eng, t + 1, 1 - slot)
                p2_pool_y(eng, t - 1, 1 - slot, ld if slot == 1 else ld - 1)
            tile_pairs(eng, body)
            p2_pool_y(eng, TILES - 2, 0, TILES // 2)
            p2_pool_y(eng, TILES - 1, 1, TILES // 2)

        def p2_dve(eng):
            for n, (src, dst, w) in enumerate(turned_weights()):
                eng.wait_ge(t_hi, n + 1)
                eng.tensor_tensor(dst[1], bank[n % 2][:, 0:w * len(src)], dst[0].bitcast(F32), ALU.subtract).then_inc(t_lo, 1)
            eng.wait_ge(t_in, T_IN)
            p2_dve_ln(eng, 0, 0, 1)
            p2_dve_ln(eng, 1, 1, 1)
            p2_dve_gate(eng, 0)
            p2_dve_u(eng, 0)

            def body(t, slot, ld):
                p2_dve_ln(eng, t + 1, 1 - slot, ld + (1 if slot == 1 else 0))
                p2_dve_gate(eng, t)
                p2_dve_y(eng, t - 1, 1 - slot, ld if slot == 1 else ld - 1)
                p2_dve_u(eng, t)
            tile_pairs(eng, body)
            t = TILES - 1
            p2_dve_gate(eng, t)
            p2_dve_y(eng, t - 1, 0, TILES // 2)
            p2_dve_u(eng, t)
            p2_dve_y(eng, t, 1, TILES // 2)

        def p2_pe(eng):
            eng.wait_ge(t_in, T_IN)
            for n, (src, dst, w) in enumerate(turned_weights()):
                if n >= 2:
                    eng.wait_ge(t_lo, n - 1)
                for j, s in enumerate(src):
                    k = s.shape[0]
                    m = eng.transpose(bank[n % 2][:, j * w:(j + 1) * w], s, ident_t[0:k, 0:k])
                m.then_inc(t_T, 1)

            def turn(t):
                eng.wait_ge(t_xn, t + 1)
                if not (isinstance(t, int) and t == 0):
                    eng.wait_ge(t_aff, 2 * t)
                for half in range(2):
                    for k in range(4 * half, 4 * half + 4):
                        m = eng.transpose(bank[6 + half][:, (k % 4) * P:(k % 4 + 1) * P], xn2[:, k * P:(k + 1) * P], ident_t[:])
                    m.then_inc(t_hT, 1)

            def up(t, slot):
                if isinstance(t, int) and t == 0:
                    eng.wait_ge(t_lo, NTURN)
                eng.wait_ge(t_h2, t + 2)
                eng.wait_ge(t_us, t + 1)
                for k in range(KT):
                    m = mm3(eng, bank[4][0:E, 0:P], sl(gT, lambda g: g[:, k, :]), sl(h2[slot], lambda h: h[:, k, :]), k == 0, k == KT - 1)
                m.then_inc(t_G, 1)
                for k in range(KT):
                    if k == KT // 2:
                        eng.wait_ge(t_lg, t + 1)
                        plain(eng.transpose(bank[3][:, 0:E], lgT[:], ident_t[0:E, 0:E])).then_inc(t_GT, 1)
                    m = mm3(eng, bank[2][:], sl(h2[slot], lambda h: h[:, k, :]), sl(aT, lambda a: a[:, k, :]), k == 0, k == KT - 1)
                m.then_inc(t_U, 1)

            def turn_u(t):
                eng.wait_ge(t_us, t + 2)
                eng.wait_ge(t_ul, t + 1)
                for cc in range(ET):
                    m = eng.transpose(bank[5][:, cc * P:(cc + 1) * P], us[:, 2 * cc:2 * cc + 2, :].rearrange("p e r -> p (e r)"), ident_t[:])
                m.then_inc(t_UT, 1)

            def down(t):
                eng.wait_ge(t_ul, t + 2)
                for half in range(2):
                    eng.wait_ge(t_y, 2 * t + half + 1)
                    for cc in range(ET):
                        m = mm3(eng, bank[half][:], sl(usT, lambda u: u[:, cc, :]), sl(bT, lambda w: w[:, cc, half * 512:(half + 1) * 512]),
                                cc == 0, cc == ET - 1)
                    m.then_inc(t_Y, 1)

            turn(0)
            up(0, 0)
            turn(1)
            turn_u(0)

            def body(t, slot, ld):
                up(t, slot)
                turn(t + 1)
                down(t - 1)
                turn_u(t)
            tile_pairs(eng, body)
            up(TILES - 1, 1)
            down(TILES - 2)
            turn_u(TILES - 1)
            down(TILES - 1)

        block = top.enter_context(nc.Block())

        @block.sync
        def _(eng):
            p0_sp(eng); phase_end(eng, 0)
            p1_sp(eng)
            for i, s in enumerate(s_stage):
                eng.wait_ge(s, 16 * (5 * GROUPS + 1 - i))
            phase_end(eng, 1)
            p2_sp(eng)
            p2_sp_tiles(eng)

        @block.gpsimd
        def _(eng):
            phase_end(eng, 0)
            p1_pool(eng); phase_end(eng, 1)
            p2_pool(eng)

        @block.scalar
        def _(eng):
            p0_act(eng); phase_end(eng, 0)
            p1_act(eng); phase_end(eng, 1)
            p2_act(eng)

        @block.vector
        def _(eng):
            p0_dve(eng); phase_end(eng, 0)
            p1_dve(eng); phase_end(eng, 1)
            for s, credit in ((t_h2, 1), (t_us, 1), (t_ul, 1), (t_UT, 1), (t_y, 2)):
                eng.sem_inc(s, credit)
            p2_dve(eng)

        @block.tensor
        def _(eng):
            p0_pe(eng); phase_end(eng, 0)
            p1_pe(eng); phase_end(eng, 1)
            p2_pe(eng)


_INS = {"L0_attn_x": "x", "L0_attn_wq": "wq", "L0_attn_wk": "wk", "L0_attn_wv": "wv", "L0_attn_wo": "wo",
        "L0_ffn_gate_w": "gate_w", "L0_ffn_lora_A": "lora_a", "L0_ffn_lora_B": "lora_b", "L0_c": "c", "L0_wmod": "wmod"}


def kernel(**inputs):
    from concourse import bacc
    from concourse.bass_utils import run_bass_kernel_spmd

    nc = bacc.Bacc("TRN2", target_bir_lowering=False, num_devices=1)
    arrays, args = {}, {}
    given = {_INS[k]: np.ascontiguousarray(v) for k, v in inputs.items()} | constants()
    for name, a in given.items():
        arrays[f"in_{name}"] = a
        args[name] = nc.dram_tensor(f"in_{name}", a.shape, mybir.dt.from_np(a.dtype), kind="ExternalInput").ap()
    args["out"] = nc.dram_tensor("out", (BATCH, SEQ, D), F32, kind="ExternalOutput").ap()
    adaln_block(nc, **args)
    r = run_bass_kernel_spmd(nc, [arrays], core_ids=[0])
    return r.results[0]["out"]
```

```python
from contextlib import ExitStack

import numpy as np

import concourse.bass as bass
from concourse import mybir

F32 = mybir.dt.float32
F32R = mybir.dt.float32r
U32 = mybir.dt.uint32
ALU = mybir.AluOpType
ACT = mybir.ActivationFunctionType

P = 128
BATCH, SEQ, D = 4, 512, 1024
HEADS, KV = 32, 8
GQ = HEADS // KV
HD = 128
WINDOW = 256
KT = D // P
QT = SEQ // P
UNITS = QT * GQ
SCALE = HD ** -0.5
EPS = 1e-5
E, R = 8, 64
ET = E * R // P
TILES = BATCH * QT
FAR = 3.0e38
NEG = -3.0e38
GROUPS = BATCH * KV
NC = 10
FAST_N = 256
LA = 3
LAG = 3
V_TURN = LA + 2


def key_tiles(i):
    return list(range(max(0, i - WINDOW // P), i + 1))


def constants():
    half = HD // 2
    inv = (np.float32(10000.0) ** (-np.arange(half, dtype=np.float32) / np.float32(half))).astype(np.float32)
    ang = inv[:, None] * np.arange(SEQ, dtype=np.float32)[None, :]
    cos, sin = np.cos(ang).astype(np.float32), np.sin(ang).astype(np.float32)
    p, j = np.arange(P)[:, None], np.arange(P)[None, :]
    mask = np.zeros((P, 3 * P), np.float32)
    mask[:, :P][~(j > p)] = NEG
    mask[:, 2 * P:][~(j <= p)] = NEG
    return {
        "cos": np.concatenate([cos, cos]),
        "sin": np.concatenate([-sin, sin]),
        "mask": mask,
        "ident": np.eye(P, dtype=np.float32),
        "iota": np.tile(np.arange(E, dtype=np.float32), (P, 1)),
    }


def adaln_block(nc, x, wq, wk, wv, wo, gate_w, lora_a, lora_b, c, wmod, cos, sin, mask, ident, iota, out):
    x_rows = x.rearrange("b s d -> (b s) d")
    out_rows = out.rearrange("b s d -> (b s) d")
    mod_d = nc.dram_tensor("mod_scratch", (6 * BATCH, D), F32, kind="Internal").ap()
    x1_d = nc.dram_tensor("x1_scratch", (BATCH * SEQ, D), F32, kind="Internal").ap()

    with ExitStack() as top:
        def sb(stack, name, shape, dt=F32):
            return stack.enter_context(nc.sbuf_tensor(name, shape, dt))

        def sem(name):
            return top.enter_context(nc.semaphore(name))

        bank = [top.enter_context(nc.psum_tensor(f"bank{i}", [P, 512], F32)) for i in range(8)]
        ident_t = sb(top, "ident_t", [P, P])
        modT = [sb(top, f"modT{l}", [P, BATCH, 2, KT]) for l in range(2)]
        modcur = sb(top, "modcur", [P, 1, 2, KT])
        barrier = sem("barrier")
        s_id = sem("s_id")

        def plain(ins):
            return ins.wait_op(s_id, 16, "sem-ge")

        def attention_end(eng):
            eng.drain().then_inc(barrier, 1)
            eng.wait_ge(barrier, 5)

        p0 = ExitStack()
        wm = [sb(p0, f"wm{i}", [P, KT, 512]) for i in range(2)]
        c_rows = sb(p0, "c_rows", [BATCH, D])
        c_sig = sb(p0, "c_sig", [BATCH, D])
        cT = sb(p0, "cT", [P, KT, BATCH])
        mrow = [sb(p0, f"mrow{i}", [BATCH, 512]) for i in range(2)]
        mabs = sb(p0, "mabs", [BATCH, 512])
        msgn = sb(p0, "msgn", [BATCH, 512])
        p0.close()
        NM = 6 * D // 512
        LN_AT = NM - KT
        s_wm = [sem(f"s_wm{i}") for i in range(2)]
        s_c0 = sem("s_c0")
        s_sig = sem("s_sig"); s_v0 = sem("s_v0"); s_ct = sem("s_ct"); s_ctc = sem("s_ctc")
        s_mm0 = sem("s_mm0"); s_mr = sem("s_mr"); s_mt = sem("s_mt"); s_mc = sem("s_mc"); s_md = [sem("s_md0"), sem("s_md1")]

        def is_gate(j):
            return (j // 2) % 3 == 2

        def p0_sp(eng):
            eng.dma_start(ident_t[:], ident).then_inc(s_id, 16)
            eng.dma_start(c_rows[:], c).then_inc(s_c0, 16)
            for j in range(NM):
                if j == 2:
                    first_loads(eng)
                if j >= 2:
                    eng.wait_ge(s_mm0, j - 1)
                eng.dma_start(wm[j % 2][:], wmod[:, j * 512:(j + 1) * 512].rearrange("(k p) n -> p k n", p=P)).then_inc(s_wm[j % 2], 16)

        def p0_act(eng):
            eng.wait_ge(s_c0, 16)
            eng.activation(c_sig[:], c_rows[:], ACT.Exp, scale=-1.0).then_inc(s_sig, 1)
            first_chunk(eng, False)
            for j in range(NM):
                eng.wait_ge(s_mm0, j + 1)
                if not is_gate(j):
                    if j >= 2 and not is_gate(j - 2):
                        eng.wait_ge(s_mt, sum(not is_gate(q) for q in range(j - 1)))
                    if j >= 2 and is_gate(j - 2):
                        eng.wait_ge(s_md[j % 2], 16 * sum(is_gate(q) for q in range(j % 2, j - 1, 2)))
                    eng.activation(mrow[j % 2][:], bank[j % 2][0:BATCH, :], ACT.Copy).then_inc(s_mr, 1)
                else:
                    eng.wait_ge(s_v0, v0_done[j])
                    q = j // 2 * BATCH
                    eng.dma_start(mod_d[q:q + BATCH, (j % 2) * 512:(j % 2 + 1) * 512], mrow[j % 2][:]).then_inc(s_md[j % 2], 16)
                if j == 3:
                    act_ln_sqrt(eng, 0)
                if j >= LN_AT:
                    act_ln_chunk(eng, 0, j - LN_AT)

        v0_done, at = {}, 3
        for j in range(NM):
            at += 6 if is_gate(j) else 1
            v0_done[j] = at

        def p0_dve(eng):
            eng.wait_ge(s_sig, 1)
            eng.tensor_scalar(c_sig[:], c_sig[:], 1.0, None, ALU.add).then_inc(s_v0, 1)
            eng.wait_ge(s_v0, 1)
            eng.reciprocal(c_sig[:], c_sig[:]).then_inc(s_v0, 1)
            eng.wait_ge(s_v0, 2)
            eng.tensor_tensor(c_rows[:], c_rows[:], c_sig[:], ALU.mult).then_inc(s_v0, 1)
            eng.wait_ge(s_ct, 1)
            eng.tensor_copy(cT[:], bank[2][:, 0:KT * BATCH].rearrange("p (k b) -> p k b", b=BATCH)).then_inc(s_ctc, 1)
            turned = 0
            for j in range(NM):
                if j == 3:
                    dve_ln_stats(eng, 0, 1, lambda t: None)
                if j == LN_AT:
                    dve_ln_normalise(eng, 0)
                part, half = divmod(j, 2)
                if is_gate(j):
                    eng.wait_ge(s_mm0, j + 1)
                    if j >= 2 and not is_gate(j - 2):
                        eng.wait_ge(s_mt, turned)
                    v = v0_done[j] - 6
                    acc = bank[j % 2][0:BATCH, :]
                    steps = [
                        lambda: eng.tensor_scalar(mabs[:], acc, -1.0, None, ALU.mult),
                        lambda: eng.tensor_tensor(mabs[:], mabs[:], acc, ALU.max),
                        lambda: eng.tensor_scalar(mabs[:], mabs[:], 0.25, None, ALU.max),
                        lambda: eng.tensor_scalar(msgn[:], acc, 0.0, 2.0, ALU.is_ge, ALU.mult),
                        lambda: eng.tensor_scalar(msgn[:], msgn[:], -1.0, None, ALU.add),
                        lambda: eng.tensor_tensor(mrow[j % 2][:], msgn[:], mabs[:], ALU.mult),
                    ]
                    for n, step in enumerate(steps):
                        eng.wait_ge(s_v0, v + n)
                        step().then_inc(s_v0, 1)
                else:
                    turned += 1
                    eng.wait_ge(s_mt, turned)
                    src = bank[2 + turned % 2][:, 0:4 * BATCH].rearrange("p (k b) -> p b k", b=BATCH)
                    dst = modT[part // 3][:, :, part % 3, half * 4:half * 4 + 4]
                    eng.tensor_scalar(dst, src, float(part % 3), None, ALU.add).then_inc(s_v0, 1)
                if j == 3:
                    eng.wait_ge(s_v0, v0_done[3])
                    dve_ln_mod(eng, 0)
                if j >= LN_AT:
                    dve_ln_chunk(eng, 0, j - LN_AT)
            eng.wait_ge(s_v0, v0_done[NM - 1])

        def p0_pe(eng):
            eng.wait_ge(s_id, 16)
            eng.wait_ge(s_v0, 3)
            for k in range(KT):
                m = eng.transpose(bank[2][:, k * BATCH:(k + 1) * BATCH], c_rows[:, k * P:(k + 1) * P], ident_t[0:BATCH, 0:BATCH])
            m.then_inc(s_ct, 1)
            eng.wait_ge(s_ctc, 1)
            turned = 0

            def turn(j):
                nonlocal turned
                if is_gate(j):
                    return
                turned += 1
                eng.wait_ge(s_mr, turned)
                if turned >= 3:
                    prev = [q for q in range(NM) if not is_gate(q)][turned - 3]
                    eng.wait_ge(s_v0, v0_done[prev])
                for k in range(4):
                    m = eng.transpose(bank[2 + turned % 2][:, k * BATCH:(k + 1) * BATCH], mrow[j % 2][:, k * P:(k + 1) * P],
                                      ident_t[0:BATCH, 0:BATCH])
                m.then_inc(s_mt, 1)

            for j in range(NM):
                eng.wait_ge(s_wm[j % 2], 16 * (j // 2 + 1))
                if j >= 2:
                    if is_gate(j - 2):
                        eng.wait_ge(s_v0, v0_done[j - 2])
                    else:
                        eng.wait_ge(s_mr, sum(not is_gate(q) for q in range(j - 1)))
                for k in range(KT):
                    m = eng.matmul(bank[j % 2][0:BATCH, :], cT[:, k, :], wm[j % 2][:, k, :], start=k == 0, stop=k == KT - 1)
                m.then_inc(s_mm0, 1)
                if j:
                    turn(j - 1)
                if j >= LN_AT:
                    pe_ln_chunk(eng, 0, j - LN_AT)
            turn(NM - 1)
            eng.wait_ge(s_v0, v0_done[NM - 2])

        p1 = ExitStack()

        def sl(pair, f):
            return tuple(f(t) for t in pair)

        def split_pair(stack, name, shape):
            return sb(stack, name + "_hi", shape, F32R), sb(stack, name + "_lo", shape, F32R)

        w_o = split_pair(p1, "w_o", [P, GQ, D])
        qo = split_pair(p1, "qo", [P, GQ, SEQ])
        kt_ = split_pair(p1, "kt_", [P, SEQ])
        v_ = split_pair(p1, "v_", [P, QT, HD])
        w_q = split_pair(p1, "w_q", [P, KT, GQ * HD])
        w_k = split_pair(p1, "w_k", [P, KT, HD])
        w_v = split_pair(p1, "w_v", [P, KT, HD])
        hT = split_pair(p1, "hT", [P, KT, SEQ])
        acc = sb(p1, "acc", [P, QT, D])
        stage = [sb(p1, f"stage{i}", [P, 1024]) for i in range(2)]
        swapped = [sb(p1, f"swapped{i}", [P, SEQ]) for i in range(2)]
        rotated = [sb(p1, f"rotated{i}", [P, SEQ]) for i in range(2)]
        prob = sb(p1, "prob", [P, GQ, 3 * P])
        cos_t = sb(p1, "cos_t", [P, SEQ])
        sin_t = sb(p1, "sin_t", [P, SEQ])
        mask_t = sb(p1, "mask_t", [P, 3 * P])
        nbias = sb(p1, "nbias", [P, UNITS])
        rowsum = sb(p1, "rowsum", [P, UNITS])
        rrow = sb(p1, "rrow", [P, UNITS])
        stats = sb(p1, "stats", [P, QT, 2, 6])
        mv = sb(p1, "mv", [P, QT, 2])
        lnv = sb(p1, "lnv", [P, 6, QT])
        with ExitStack() as a:
            pT = [split_pair(a, f"pT{i}", [P, 3, GQ * P]) for i in range(2)]
        with ExitStack() as a:
            xb = sb(a, "xb", [P, QT, D])
            ga_t = sb(a, "ga_t", [P, D])
        p1.close()

        s_cst = sem("s_cst")
        s_stage = [sem("s_stage0"), sem("s_stage1")]
        s_split = sem("s_split")
        s_proj = sem("s_proj")
        s_wo = sem("s_wo")
        s_act = sem("s_act")
        s_dve = sem("s_dve")
        s_swp = sem("s_swp"); s_rs = sem("s_rs"); s_ra = sem("s_ra"); s_rh = sem("s_rh")
        s_qk = sem("s_qk")
        s_vt = sem("s_vt"); s_vh = sem("s_vh"); s_v = sem("s_v")
        s_S = sem("s_S"); s_msk = sem("s_msk"); s_exp = sem("s_exp"); s_rl = sem("s_rl"); s_nrm = [sem(f"s_nrm{h}") for h in range(GQ)]
        s_T = sem("s_T"); s_pth = sem("s_pth"); s_ptl = sem("s_ptl"); s_pv = sem("s_pv"); s_oh = sem("s_oh"); s_ol = sem("s_ol")
        s_xb = [sem(f"s_xb{t}") for t in range(QT)]
        s_ga = sem("s_ga"); s_x1 = sem("s_x1")
        s_ln = sem("s_ln"); s_sq = sem("s_sq"); s_xn = sem("s_xn"); s_lnT = sem("s_lnT"); s_lna = sem("s_lna"); s_lnh = sem("s_lnh"); s_h = sem("s_h")
        s_fin = sem("s_fin"); s_acc0 = sem("s_acc0"); s_mc1 = sem("s_mc1")

        LN_STEPS = 3 * QT + 8
        s_wor = sem("s_wor")

        def bank_free(eng, n, name):
            before = {"Q1": 1, "Q2": 2, "Q3": 3, "V": 4}
            if name in before:
                eng.wait_ge(s_rs, 5 * n + before[name])

        def chunk_source(j, g):
            if j == 0 or j == 5:
                w = wv if j == 0 else wk
                return w[:, bass.ds(g * HD, HD)].rearrange("(k p) n -> p k n", p=P), "p (k n) -> p k n", dict(n=HD)
            if j <= 4:
                k = 2 * (j - 1)
                return wq[k * P:(k + 2) * P, bass.ds(g * GQ * HD, GQ * HD)].rearrange("(k p) n -> p k n", p=P), "p (k n) -> p k n", dict(k=2)
            return wo[bass.ds(g * GQ * HD + (j - 6) * HD, HD), :], None, None

        def load_chunk(eng, slot, j, g):
            src, pat, kw = chunk_source(j, g)
            dst = stage[slot][:]
            if pat:
                dst = dst.rearrange(pat, **kw)
            eng.dma_start(dst, src).then_inc(s_stage[slot], 16)

        def first_loads(eng):
            for t, src in ((cos_t, cos), (sin_t, sin), (mask_t, mask)):
                eng.dma_start(t[:], src).then_inc(s_cst, 16)
            load_chunk(eng, 0, 5, 0)

        def p1_sp(eng):
            with eng.Fori(0, GROUPS) as n:
                for j in range(NC):
                    eng.wait_ge(s_split, 10 * n + j + 1)
                    load_chunk(eng, (1 + j) % 2, j, (n + 1) % KV if j == 5 else n % KV)

        s_hi = sem("s_hi")

        def chunk(j):
            slot = (1 + j) % 2
            if j == 0:
                dst = sl(w_v, lambda w: w[:])
            elif j <= 4:
                dst = sl(w_q, lambda w: w[:, 2 * (j - 1):2 * j, :])
            elif j == 5:
                dst = sl(w_k, lambda w: w[:])
            else:
                dst = sl(w_o, lambda w: w[:, j - 6, :])
            src = stage[slot][:]
            if len(dst[0].shape) == 3:
                src = src.rearrange("p (k n) -> p k n", n=dst[0].shape[2])
            return slot, dst, src

        def act_chunk(eng, n, j):
            slot, dst, src = chunk(j)
            if j == 0:
                eng.wait_ge(s_proj, 6 * n + 1)
            elif j == 5:
                eng.wait_ge(s_proj, 6 * n + 2)
            elif j == 6:
                eng.wait_ge(s_wo, 8 * n + 1)
            eng.wait_ge(s_stage[slot], 16 * (5 * n + (1 + j) // 2 + 1))
            eng.activation(dst[0], src, ACT.Copy).then_inc(s_hi, 1)

        def pool_chunk(eng, n, j):
            slot, dst, src = chunk(j)
            eng.wait_ge(s_hi, 10 * n + j + 2)
            eng.tensor_tensor(dst[1], src, dst[0].bitcast(F32), ALU.subtract).then_inc(s_split, 1)

        def first_chunk(eng, pool):
            slot, dst, src = chunk(5)
            if pool:
                eng.wait_ge(s_hi, 1)
                eng.tensor_tensor(dst[1], src, dst[0].bitcast(F32), ALU.subtract).then_inc(s_split, 1)
            else:
                eng.wait_ge(s_stage[slot], 16)
                eng.activation(dst[0], src, ACT.Copy).then_inc(s_hi, 1)

        def p1_pool(eng):
            first_chunk(eng, True)
            with eng.Fori(0, GROUPS) as n:
                for j in range(NC):
                    pool_chunk(eng, n, j)

        def mm3(eng, o, st, mv_, start, stop):
            eng.matmul(o, st[0], mv_[0], start=start, stop=False)
            eng.matmul(o, st[0], mv_[1], start=False, stop=False)
            return eng.matmul(o, st[1], mv_[0], start=False, stop=stop)

        def pe_project(eng, n, name, w, cols, bk, waits):
            bank_free(eng, n, name)
            for k in range(KT):
                if k in waits:
                    eng.wait_ge(*waits[k])
                m = mm3(eng, bank[bk][:], sl(w, lambda t: t[:, k, cols]), sl(hT, lambda t: t[:, k, :]), k == 0, k == KT - 1)
            m.then_inc(s_proj, 1)

        SBANK = [bank[2], bank[3], bank[4]]

        def pe_wo(eng, n, half):
            t, c = divmod(half, 2)
            if half == 0:
                eng.wait_ge(s_split, 10 * n + 12)
            if c == 0:
                eng.wait_ge(s_ol, QT * n + t + 1)
            if half >= 3:
                eng.wait_ge(s_wor, 8 * n + half - 1)
            for h in range(GQ):
                m = mm3(eng, SBANK[half % 3][:], sl(qo, lambda q: q[:, h, t * P:(t + 1) * P]),
                        sl(w_o, lambda w: w[:, h, c * 512:(c + 1) * 512]), h == 0, h == GQ - 1)
            m.then_inc(s_wo, 1)

        OBANK = [bank[7], bank[1]]

        def pe_scores(eng, n, u):
            i, h = divmod(u, GQ)
            kts = key_tiles(i)
            if i == 0:
                eng.wait_ge(s_qk, 5 * n + 2 + h)
            if u >= 3:
                eng.wait_ge(s_msk, UNITS * n + u - 2)
            cols = max(P * len(kts), FAST_N)
            mm3(eng, SBANK[u % 3][:, 0:cols], sl(qo, lambda q: q[:, h, i * P:(i + 1) * P]),
                sl(kt_, lambda k: k[:, kts[0] * P:kts[0] * P + cols]), True, True).then_inc(s_S, 1)

        def pe_turn(eng, n, u):
            eng.wait_ge(s_nrm[u % GQ], QT * n + u // GQ + 1)
            if u >= 2:
                eng.wait_ge(s_ptl, UNITS * n + u - 1)
            for b in range(len(key_tiles(u // GQ))):
                m = eng.transpose(bank[5 + u % 2][:, b * P:(b + 1) * P], prob[:, u % GQ, b * P:(b + 1) * P], ident_t[:])
            m.then_inc(s_T, 1)

        def pe_values(eng, n, i):
            eng.wait_ge(s_ptl, UNITS * n + GQ * (i + 1))
            if i == 0:
                eng.wait_ge(s_v, n + 2)
            elif i >= 2:
                eng.wait_ge(s_ol, QT * n + i - 1)
            kts = key_tiles(i)
            for b, kt in enumerate(kts):
                m = mm3(eng, OBANK[i % 2][:], sl(v_, lambda v: v[:, kt, :]), sl(pT[i % 2], lambda p: p[:, b, :]), b == 0, b == len(kts) - 1)
            m.then_inc(s_pv, 1)

        K_AT = (1, 2, 3, 4, 5, 6, 13, 14)

        def pe_attention(eng, n, next_k):
            for u in range(UNITS):
                if u + LA < UNITS:
                    pe_scores(eng, n, u + LA)
                if next_k and u in K_AT:
                    k = K_AT.index(u)
                    if k == 0:
                        eng.wait_ge(s_split, 10 * n + 8)
                    m = mm3(eng, bank[0][:], sl(w_k, lambda t: t[:, k, :]), sl(hT, lambda t: t[:, k, :]), k == 0, k == KT - 1)
                    if k == KT - 1:
                        m.then_inc(s_proj, 1)
                pe_turn(eng, n, u)
                if u == 1:
                    eng.wait_ge(s_act, 7 * n + 6)
                    for t in range(QT):
                        m = eng.transpose(bank[7][:, t * P:(t + 1) * P], swapped[1][:, t * P:(t + 1) * P], ident_t[:])
                    m.then_inc(s_vt, 1)
                if u % GQ == 1 and GQ < u < UNITS - GQ:
                    pe_values(eng, n, u // GQ - 1)
            for i in (QT - 2, QT - 1):
                pe_values(eng, n, i)

        def pe_first_k(eng, n, b):
            eng.wait_ge(s_wor, 8 * n + 1)
            eng.wait_ge(s_split, 10 * n + 2)
            for k in range(KT):
                eng.wait_ge(s_h, KT * b + k + 1)
                m = mm3(eng, bank[0][:], sl(w_k, lambda t: t[:, k, :]), sl(hT, lambda t: t[:, k, :]), k == 0, k == KT - 1)
            m.then_inc(s_proj, 1)

        def pe_qv(eng, n):
            for h in range(GQ):
                waits = {2 * q: (s_split, 10 * n + 4 + q) for q in range(4)} if h == 0 else {}
                pe_project(eng, n, f"Q{h}", w_q, slice(h * HD, (h + 1) * HD), 1 - h % 2, waits)
            eng.wait_ge(s_wor, 8 * n + 1)
            for u in range(LA):
                pe_scores(eng, n, u)
            pe_project(eng, n, "V", w_v, slice(0, HD), 1, {})

        def pe_ln_chunk(eng, b1, k):
            if k == 0:
                eng.wait_ge(s_xn, QT * b1 + QT)
            if k >= 2:
                eng.wait_ge(s_lna, KT * b1 + k - 1)
            for t in range(QT):
                m = eng.transpose(bank[5 + k % 2][:, t * P:(t + 1) * P], xb[:, t, k * P:(k + 1) * P], ident_t[:])
            m.then_inc(s_lnT, 1)

        def p1_pe(eng):
            last = BATCH - 1
            pe_first_k(eng, 0, 0)
            eng.wait_ge(s_v0, v0_done[NM - 1])
            pe_qv(eng, 0)
            with eng.Fori(0, last) as b:
                pe_groups(eng, b)
                n = b * KV + (KV - 1)
                for half in range(6):
                    pe_wo(eng, n, half)
                for k in range(KT):
                    pe_ln_chunk(eng, b + 1, k)
                for half in range(6, 8):
                    pe_wo(eng, n, half)
                pe_first_k(eng, n + 1, b + 1)
                pe_qv(eng, n + 1)
            pe_groups(eng, last)
            for half in range(8):
                pe_wo(eng, GROUPS - 1, half)

        def pe_groups(eng, b):
            with eng.Fori(1, KV) as g:
                n = b * KV + g
                pe_attention(eng, n - 1, True)
                for half in range(8):
                    pe_wo(eng, n - 1, half)
                pe_qv(eng, n)
            pe_attention(eng, b * KV + (KV - 1), False)

        OUT_STEP = {GQ * i + GQ + 1 + LAG: i for i in range(QT - 2)}

        def act_rope(eng, n, r):
            slot = r % 2
            eng.wait_ge(s_dve, 5 * n + r + 1)
            if r >= 2:
                eng.wait_ge(s_qk, 5 * n + r - 1)
            half = HD // 2
            bk = bank[0 if r % 2 == 0 else 1]
            eng.activation(swapped[slot][0:half, :], bk[half:HD, :], ACT.Copy)
            eng.activation(swapped[slot][half:HD, :], bk[0:half, :], ACT.Copy).then_inc(s_act, 1)
            if r:
                act_chunk(eng, n, 5 + r)
            dst = kt_[0][:] if r == 0 else qo[0][:, r - 1, :]
            eng.wait_ge(s_ra, 5 * n + r + 1)
            eng.activation(dst, rotated[slot][:], ACT.Copy).then_inc(s_rh, 1)

        def act_project(eng, n, batch_done=None):
            early = 2 if batch_done is None else 4
            for j in range(early):
                act_chunk(eng, n, j)
            act_rope(eng, n, 0)
            for j in range(early, 6):
                act_chunk(eng, n, j)
            if batch_done is not None:
                act_store_x1(eng, batch_done)
            for r in range(1, 1 + GQ):
                act_rope(eng, n, r)

        def act_attention(eng, n, b):
            for s in range(UNITS + LAG):
                if s == LA:
                    eng.wait_ge(s_proj, 6 * n + 7)
                    eng.wait_ge(s_qk, 5 * n + 4)
                    eng.activation(swapped[1][:], bank[1][:], ACT.Copy).then_inc(s_act, 1)
                if s == V_TURN:
                    eng.wait_ge(s_vt, n + 1)
                    eng.activation(v_[0][:], bank[7][:].rearrange("p (t d) -> p t d", d=HD), ACT.Copy).then_inc(s_act, 1)
                u = s - LAG
                if 0 <= u < UNITS:
                    i, h = divmod(u, GQ)
                    eng.wait_ge(s_T, UNITS * n + u + 1)
                    if h == 0 and i >= 2:
                        eng.wait_ge(s_pv, QT * n + i - 1)
                    if u == 0:
                        eng.wait_ge(s_x1, 16 * QT * b + 16)
                    nk = len(key_tiles(i))
                    eng.activation(pT[i % 2][0][:, 0:nk, h * P:(h + 1) * P],
                                   bank[5 + u % 2][:, 0:nk * P].rearrange("p (b q) -> p b q", q=P), ACT.Copy).then_inc(s_pth, 1)
                if s < UNITS:
                    w = P * len(key_tiles(s // GQ))
                    tile = prob[:, s % GQ, 0:w]
                    eng.wait_ge(s_msk, UNITS * n + s + 1)
                    eng.activation(tile, tile, ACT.Exp, bias=nbias[:, s:s + 1], scale=-1.0,
                                   accum_out=rowsum[:, s:s + 1]).then_inc(s_exp, 1)
                if s in OUT_STEP:
                    act_outputs(eng, n, OUT_STEP[s])
            for i in (QT - 2, QT - 1):
                act_outputs(eng, n, i)

        def act_outputs(eng, n, i):
            eng.wait_ge(s_pv, QT * n + i + 1)
            eng.activation(qo[0][:, :, i * P:(i + 1) * P], OBANK[i % 2][:].rearrange("p (h q) -> p h q", q=P), ACT.Copy).then_inc(s_oh, 1)

        def act_load_x(eng, b, tiles):
            for t in tiles:
                eng.dma_start(xb[:, t, :], x_rows[bass.ds(b * SEQ + t * P, P), :]).then_inc(s_xb[t], 16)

        def act_ln_sqrt(eng, b1):
            eng.wait_ge(s_ln, LN_STEPS * b1 + LN_VAR)
            eng.activation(lnv[:, 1, :], lnv[:, 0, :], ACT.Sqrt).then_inc(s_sq, 1)

        def act_ln_chunk(eng, b1, k):
            eng.wait_ge(s_lnT, KT * b1 + k + 1)
            if k == 0:
                eng.wait_ge(s_mc1, b1 + 1)
            if k >= 2:
                eng.wait_ge(s_h, KT * b1 + k - 1)
            eng.activation(rotated[k % 2][:], bank[5 + k % 2][:], ACT.Identity, bias=modcur[:, 0, 0, k:k + 1],
                           scale=modcur[:, 0, 1, k:k + 1]).then_inc(s_lna, 1)
            eng.wait_ge(s_lna, KT * b1 + k + 1)
            eng.activation(hT[0][:, k, :], rotated[k % 2][:], ACT.Copy).then_inc(s_lnh, 1)

        def p1_act(eng):
            last = BATCH - 1
            for i in range(2):
                eng.wait_ge(s_md[i], 16 * sum(is_gate(q) for q in range(i, NM, 2)))
            act_project(eng, 0)
            with eng.Fori(0, last) as b:
                act_groups(eng, b)
                act_load_x(eng, b + 1, range(QT))
                act_load_ga(eng, b)
                act_ln_sqrt(eng, b + 1)
                for k in range(KT):
                    act_ln_chunk(eng, b + 1, k)
                act_load_x(eng, b, range(QT))
                act_project(eng, (b + 1) * KV, b)
            act_groups(eng, last)
            act_load_x(eng, last, range(QT))
            act_load_ga(eng, last)
            act_store_x1(eng, last)
            eng.wait_ge(s_x1, 16 * TILES + 16)

        def act_groups(eng, b):
            with eng.Fori(1, KV) as g:
                n = b * KV + g
                act_attention(eng, n - 1, b)
                act_project(eng, n)
            act_attention(eng, b * KV + (KV - 1), b)

        def act_load_ga(eng, b):
            eng.dma_start(ga_t[:], mod_d[bass.ds(2 * BATCH + b, 1), :].broadcast_to([P, D])).then_inc(s_ga, 16)

        def act_store_x1(eng, b):
            for t in range(QT):
                eng.wait_ge(s_fin, 2 * QT * b + 2 * t + 2)
                eng.dma_start(x1_d[bass.ds(b * SEQ + t * P, P), :], xb[:, t, :]).then_inc(s_x1, 16)

        LN_VAR = 3 * QT + 1

        def dve_rope(eng, n, r):
            slot = r % 2
            bk = bank[0 if r % 2 == 0 else 1]
            eng.wait_ge(s_proj, 6 * n + 2 + r)
            eng.tensor_tensor(rotated[slot][:], bk[:], cos_t[:], ALU.mult).then_inc(s_dve, 1)
            eng.wait_ge(s_act, 7 * n + r + 1)
            eng.tensor_tensor(swapped[slot][:], swapped[slot][:], sin_t[:], ALU.mult).then_inc(s_rs, 1)
            eng.wait_ge(s_rs, 5 * n + r + 1)
            eng.wait_ge(s_dve, 5 * n + r + 1)
            eng.tensor_tensor(rotated[slot][:], rotated[slot][:], swapped[slot][:], ALU.add).then_inc(s_ra, 1)
            eng.wait_ge(s_rh, 5 * n + r + 1)
            eng.wait_ge(s_ra, 5 * n + r + 1)
            hi, lo = (kt_[0][:], kt_[1][:]) if r == 0 else (qo[0][:, r - 1, :], qo[1][:, r - 1, :])
            eng.tensor_tensor(lo, rotated[slot][:], hi.bitcast(F32), ALU.subtract).then_inc(s_qk, 1)

        def dve_wo(eng, n, half):
            t, cc = divmod(half, 2)
            eng.wait_ge(s_wo, 8 * n + half + 2)
            a = acc[:, t, cc * 512:(cc + 1) * 512]
            eng.tensor_tensor(a, SBANK[half % 3][:], a, ALU.add).then_inc(s_wor, 1)

        def dve_outputs(eng, n, i):
            eng.wait_ge(s_oh, QT * n + i + 1)
            o = OBANK[i % 2][:].rearrange("p (h q) -> p h q", q=P)
            eng.tensor_tensor(qo[1][:, :, i * P:(i + 1) * P], o, qo[0][:, :, i * P:(i + 1) * P].bitcast(F32),
                              ALU.subtract).then_inc(s_ol, 1)

        def dve_attention(eng, n):
            for s in range(UNITS + LAG):
                if s < UNITS:
                    w = P * len(key_tiles(s // GQ))
                    eng.wait_ge(s_S, UNITS * n + s + 1)
                    if s >= GQ:
                        eng.wait_ge(s_T, UNITS * n + s - GQ + 1)
                    plain(eng.tensor_tensor_reduce(prob[:, s % GQ, 0:w], SBANK[s % 3][:, 0:w], mask_t[:, 3 * P - w:3 * P], -SCALE, FAR,
                                             ALU.add, ALU.min, nbias[:, s:s + 1])).then_inc(s_msk, 1)
                u = s - LAG
                if 0 <= u < UNITS:
                    i, h = divmod(u, GQ)
                    nk = len(key_tiles(i))
                    eng.wait_ge(s_pth, UNITS * n + u + 1)
                    hi, lo = (p[:, 0:nk, h * P:(h + 1) * P] for p in pT[i % 2])
                    eng.tensor_tensor(lo, bank[5 + u % 2][:, 0:nk * P].rearrange("p (b q) -> p b q", q=P), hi.bitcast(F32),
                                      ALU.subtract).then_inc(s_ptl, 1)
                if 1 <= s < UNITS + 1:
                    eng.wait_ge(s_exp, UNITS * n + s)
                    eng.reciprocal(rrow[:, s - 1:s], rowsum[:, s - 1:s]).then_inc(s_rl, 1)
                    eng.wait_ge(s_rl, UNITS * n + s)
                    tile = prob[:, (s - 1) % GQ, 0:P * len(key_tiles((s - 1) // GQ))]
                    eng.tensor_scalar(tile, tile, rrow[:, s - 1:s], None, ALU.mult).then_inc(s_nrm[(s - 1) % GQ], 1)
                if s == V_TURN:
                    eng.wait_ge(s_act, 7 * n + 7)
                    eng.tensor_tensor(v_[1][:], bank[7][:].rearrange("p (t d) -> p t d", d=HD), v_[0][:].bitcast(F32),
                                      ALU.subtract).then_inc(s_v, 1)
                if s - 1 in OUT_STEP:
                    dve_outputs(eng, n, OUT_STEP[s - 1])
            for i in (QT - 2, QT - 1):
                dve_outputs(eng, n, i)

        def ln_ops(eng, xt, st, mv_, lv, steps, base, semaphore, ntile, wait_x, wait_sq, fill):
            cnt = [0]

            def do(ins):
                cnt[0] += 1
                ins.then_inc(semaphore, 1)

            def after():
                eng.wait_ge(semaphore, base + cnt[0])

            for t in range(ntile):
                wait_x(t)
                do(plain(eng.bn_stats(st[:, t, 0, :], xt(t)[:, 0:512])))
                do(eng.bn_stats(st[:, t, 1, :], xt(t)[:, 512:1024]))
                after()
                do(plain(eng.bn_aggr(mv_[:, t, :], st[:, t, :, :].rearrange("p a s -> p (a s)"))))
                fill(t)
            after()
            do(eng.tensor_scalar(lv[:, 0, :], mv_[:, :, 1], EPS, None, ALU.add))
            wait_sq()
            do(eng.reciprocal(lv[:, 1, :], lv[:, 1, :])); after()
            do(eng.tensor_tensor(lv[:, 2, :], lv[:, 1, :], lv[:, 1, :], ALU.mult)); after()
            do(eng.tensor_tensor(lv[:, 2, :], lv[:, 2, :], lv[:, 0, :], ALU.mult)); after()
            do(eng.tensor_scalar(lv[:, 2, :], lv[:, 2, :], -0.5, 1.5, ALU.mult, ALU.add)); after()
            do(eng.tensor_tensor(lv[:, 3, :], lv[:, 2, :], lv[:, 1, :], ALU.mult)); after()
            do(eng.tensor_scalar(lv[:, 4, :], mv_[:, :, 0], -1.0, None, ALU.mult)); after()
            do(eng.tensor_tensor(lv[:, 5, :], lv[:, 4, :], lv[:, 3, :], ALU.mult)); after()
            assert cnt[0] == steps, cnt

        def dve_ln_mod(eng, b):
            eng.tensor_copy(modcur[:, 0, :, :], modT[0][:, bass.ds(b, 1), :, :].rearrange("p o s k -> p (o s) k")).then_inc(s_mc1, 1)

        def dve_ln_stats(eng, b1, xloads, fill):
            ln_ops(eng, lambda t: xb[:, t, :], stats, mv, lnv, LN_STEPS, LN_STEPS * b1, s_ln, QT,
                   lambda t: eng.wait_ge(s_xb[t], 16 * xloads), lambda: eng.wait_ge(s_sq, b1 + 1), fill)

        def dve_ln_normalise(eng, b1):
            for t in range(QT):
                eng.tensor_scalar(xb[:, t, :], xb[:, t, :], lnv[:, 3, t:t + 1], lnv[:, 5, t:t + 1], ALU.mult, ALU.add).then_inc(s_xn, 1)

        def dve_ln_chunk(eng, b1, k):
            eng.wait_ge(s_lnh, KT * b1 + k + 1)
            eng.tensor_tensor(hT[1][:, k, :], rotated[k % 2][:], hT[0][:, k, :].bitcast(F32), ALU.subtract).then_inc(s_h, 1)

        def p1_dve(eng):
            eng.memset(acc[:], 0.0).then_inc(s_acc0, 1)
            eng.wait_ge(s_cst, 48)
            last = BATCH - 1
            for r in range(1 + GQ):
                dve_rope(eng, 0, r)
            with eng.Fori(0, last) as b:
                dve_groups(eng, b)
                n = b * KV + (KV - 1)
                dve_ln_mod(eng, b + 1)
                dve_ln_stats(eng, b + 1, 2 * b + 2, lambda t: dve_wo(eng, n, t))
                dve_ln_normalise(eng, b + 1)
                dve_wo(eng, n, 4)
                dve_wo(eng, n, 5)
                for k in range(KT):
                    dve_ln_chunk(eng, b + 1, k)
                dve_wo(eng, n, 6)
                dve_wo(eng, n, 7)
                for t in range(QT):
                    if t == QT // 2:
                        dve_rope(eng, n + 1, 0)
                    dve_residual(eng, b, t, 2 * b + 3)
                dve_rope(eng, n + 1, 1)
                dve_rope(eng, n + 1, 2)
                eng.wait_ge(s_fin, 2 * QT * b + 2 * QT)
                eng.memset(acc[:], 0.0).then_inc(s_acc0, 1)
                dve_rope(eng, n + 1, 3)
                dve_rope(eng, n + 1, 4)
            dve_groups(eng, last)
            for half in range(8):
                dve_wo(eng, GROUPS - 1, half)
            for t in range(QT):
                dve_residual(eng, last, t, 2 * last + 2)

        def dve_groups(eng, b):
            with eng.Fori(1, KV) as g:
                n = b * KV + g
                dve_attention(eng, n - 1)
                eng.wait_ge(s_acc0, b + 1)
                dve_wo(eng, n - 1, 0)
                dve_rope(eng, n, 0)
                for half in range(1, 8):
                    dve_wo(eng, n - 1, half)
                for r in range(1, 1 + GQ):
                    dve_rope(eng, n, r)
            dve_attention(eng, b * KV + (KV - 1))

        def dve_residual(eng, b, t, xloads):
            if t == 0:
                eng.wait_ge(s_ga, 16 * b + 16)
            eng.wait_ge(s_wor, 8 * KV * (b + 1) + 1)
            eng.tensor_tensor(acc[:, t, :], acc[:, t, :], ga_t[:], ALU.mult).then_inc(s_fin, 1)
            eng.wait_ge(s_fin, 2 * QT * b + 2 * t + 1)
            eng.wait_ge(s_xb[t], 16 * xloads)
            eng.tensor_tensor(xb[:, t, :], xb[:, t, :], acc[:, t, :], ALU.add).then_inc(s_fin, 1)

        p2 = ExitStack()
        SLOTS = 4

        def tile_slot(buf, t):
            return buf[:, bass.ds(t % SLOTS, 1), :].rearrange("p o d -> p (o d)")

        x1 = sb(p2, "x1", [P, SLOTS, D])
        gb = sb(p2, "gb", [P, SLOTS, D])
        h2 = [split_pair(p2, f"h2{i}", [P, KT, P]) for i in range(2)]
        hf = sb(p2, "hf", [P, KT, P])
        xn2 = sb(p2, "xn2", [P, D])
        a_in = sb(p2, "a_in", [P, ET, D])
        b_in = sb(p2, "b_in", [P, KT, E, R])
        g_in = sb(p2, "g_in", [E, D])
        iota_t = sb(p2, "iota_t", [P, E])
        aT = split_pair(p2, "aT", [P, KT, E * R])
        bT = split_pair(p2, "bT", [P, ET, D])
        gT = split_pair(p2, "gT", [P, KT, E])
        us = sb(p2, "us", [P, E, R])
        usT = split_pair(p2, "usT", [P, ET, P])
        yo = sb(p2, "yo", [P, D])
        mod2 = [sb(p2, f"mod2{i}", [P, 2, KT]) for i in range(2)]
        st2 = sb(p2, "st2", [P, 1, 2, 6])
        mv2 = sb(p2, "mv2", [P, 1, 2])
        lnv2 = sb(p2, "lnv2", [P, 6, 1])
        lgT = sb(p2, "lgT", [E, P])
        logit = sb(p2, "logit", [P, E])
        top8 = sb(p2, "top8", [P, E])
        idx8 = sb(p2, "idx8", [P, E], U32)
        idxf = sb(p2, "idxf", [P, E])
        gv = sb(p2, "gv", [P, 8])
        oneh = sb(p2, "oneh", [P, 2, E])
        wfull = sb(p2, "wfull", [P, E])
        p2.close()

        t_in = sem("t_in"); t_T = sem("t_T"); t_hi = sem("t_hi"); t_lo = sem("t_lo")
        t_x1 = [sem("t_x10"), sem("t_x11")]; t_gb = [sem("t_gb0"), sem("t_gb1")]
        t_ln = sem("t_ln"); t_sq = sem("t_sq"); t_xn = sem("t_xn"); t_hT = sem("t_hT"); t_aff = sem("t_aff")
        t_h2h = sem("t_h2h"); t_h2 = sem("t_h2"); t_mc = sem("t_mc")
        t_lg = sem("t_lg"); t_GT = sem("t_GT"); t_hfree = sem("t_hfree"); t_ya = sem("t_ya")
        t_U = sem("t_U"); t_G = sem("t_G"); t_gate = sem("t_gate"); t_e = sem("t_e"); t_us = sem("t_us"); t_UT = sem("t_UT")
        t_uh = sem("t_uh"); t_ul = sem("t_ul"); t_Y = sem("t_Y"); t_y = sem("t_y"); t_out = sem("t_out")
        NTURN = KT + 2 * ET + 1
        LN2_STEPS = 3 + 8
        GATE = 9

        def turned_weights():
            for k in range(KT):
                yield [a_in[:, cc, k * P:(k + 1) * P] for cc in range(ET)], sl(aT, lambda a: a[:, k, :]), P
            for cc in range(ET):
                for half in range(2):
                    yield [b_in[:, 4 * half + j, 2 * cc:2 * cc + 2, :].rearrange("p e r -> p (e r)") for j in range(4)], \
                        sl(bT, lambda w: w[:, cc, half * 512:(half + 1) * 512]), P
            yield [g_in[:, k * P:(k + 1) * P] for k in range(KT)], sl(gT, lambda g: g[:].rearrange("p k e -> p (k e)")), E

        def p2_sp(eng):
            eng.wait_ge(s_proj, 6 * GROUPS + 1)
            eng.dma_start(a_in[:], lora_a.rearrange("(c e) r d -> (e r) c d", e=2)).then_inc(t_in, 16)
            for e in range(E):
                eng.dma_start(b_in[:, :, e, :], lora_b[e].rearrange("(k p) r -> p k r", p=P)).then_inc(t_in, 16)
            eng.dma_start(g_in[:], gate_w).then_inc(t_in, 16)
            eng.dma_start(iota_t[:], iota).then_inc(t_in, 16)

        def p2_sp_tiles(eng):
            eng.sem_inc(t_out, 16)
            for t in range(3):
                if t == 2:
                    eng.wait_ge(t_x1[0], 16)
                    eng.wait_ge(t_gb[0], 16)
                p2_load(eng, t, t % 2)

            def body(t, slot, ld):
                eng.wait_ge(t_x1[slot], 16 * ld)
                eng.wait_ge(t_gb[slot], 16 * ld)
                p2_load(eng, t + 2, slot)
                p2_store(eng, t - 1)
            tile_pairs(eng, body)
            for t in (TILES - 2, TILES - 1):
                p2_store(eng, t)
            for s in (t_x1[0], t_gb[0]):
                eng.wait_ge(s, 16 * (TILES // 2 + 1))
            eng.wait_ge(t_out, 16 * TILES + 16)

        T_IN = 16 * (3 + E)

        def p2_load(eng, t, slot):
            eng.dma_start(tile_slot(x1, t), x1_d[bass.ds(t % TILES * P, P), :]).then_inc(t_x1[slot], 16)
            eng.dma_start(tile_slot(gb, t), mod_d[bass.ds(5 * BATCH + t % TILES // QT, 1), :].broadcast_to([P, D])).then_inc(t_gb[slot], 16)

        def tile_pairs(eng, body):
            with eng.Fori(0, TILES // 2 - 1) as q:
                for z in range(2):
                    body(2 * q + 1 + z, (1 + z) % 2, q + (1 if z == 0 else 2))

        def p2_act_ln(eng, t, slot):
            eng.wait_ge(t_ln, LN2_STEPS * t + 4)
            eng.activation(lnv2[:, 1, :], lnv2[:, 0, :], ACT.Sqrt).then_inc(t_sq, 1)

        def p2_act_h(eng, t, slot):
            for half in range(2):
                eng.wait_ge(t_hT, 2 * t + half + 1)
                if half == 0:
                    eng.wait_ge(t_mc, t + 1)
                    eng.wait_ge(t_h2, t + 1)
                for k in range(4 * half, 4 * half + 4):
                    ins = eng.activation(hf[:, k, :], bank[6 + half][:, (k % 4) * P:(k % 4 + 1) * P], ACT.Identity,
                                         bias=mod2[slot][:, 0, k:k + 1], scale=mod2[slot][:, 1, k:k + 1])
                ins.then_inc(t_aff, 1)
            eng.wait_ge(t_aff, 2 * t + 2)
            eng.activation(h2[slot][0][:], hf[:], ACT.Copy).then_inc(t_h2h, 1)

        def p2_act_mid(eng, t):
            eng.wait_ge(t_G, t + 1)
            eng.activation(lgT[:], bank[4][0:E, 0:P], ACT.Copy).then_inc(t_lg, 1)
            eng.wait_ge(t_gate, GATE * t + 4)
            eng.activation(gv[:, 1:2], gv[:, 0:1], ACT.Exp).then_inc(t_e, 1)

        def p2_act_u(eng, t):
            eng.wait_ge(t_UT, t + 2)
            eng.activation(usT[0][:], bank[5][:].rearrange("p (c q) -> p c q", q=P), ACT.Copy).then_inc(t_uh, 1)

        def p2_store(eng, t):
            eng.wait_ge(t_ya, 2 * t + 2)
            eng.dma_start(out_rows[bass.ds(t * P, P), :], yo[:]).then_inc(t_out, 16)

        def p2_act(eng):
            for n, (src, dst, w) in enumerate(turned_weights()):
                eng.wait_ge(t_T, n + 1)
                eng.activation(dst[0], bank[n % 2][:, 0:w * len(src)], ACT.Copy).then_inc(t_hi, 1)
            p2_act_ln(eng, 0, 0)
            p2_act_h(eng, 0, 0)
            p2_act_ln(eng, 1, 1)
            p2_act_mid(eng, 0)
            p2_act_h(eng, 1, 1)
            p2_act_u(eng, 0)

            def body(t, slot, ld):
                p2_act_ln(eng, t + 1, 1 - slot)
                p2_act_mid(eng, t)
                p2_act_h(eng, t + 1, 1 - slot)
                p2_act_u(eng, t)
            tile_pairs(eng, body)
            t = TILES - 1
            p2_act_mid(eng, t)
            p2_act_u(eng, t)

        def p2_dve_ln(eng, t, slot, ld):
            eng.tensor_copy(mod2[slot][:], modT[1][:, bass.ds(t // QT, 1), :, :].rearrange("p o s k -> p (o s) k")).then_inc(t_mc, 1)
            x1s = tile_slot(x1, t)
            ln_ops(eng, lambda _: x1s, st2, mv2, lnv2, LN2_STEPS, LN2_STEPS * t, t_ln, 1,
                   lambda _: eng.wait_ge(t_x1[slot], 16 * ld), lambda: eng.wait_ge(t_sq, t + 1), lambda _: None)
            if not (isinstance(t, int) and t == 0):
                eng.wait_ge(t_hT, 2 * t)
            eng.tensor_scalar(xn2[:], x1s, lnv2[:, 3, 0:1], lnv2[:, 5, 0:1], ALU.mult, ALU.add).then_inc(t_xn, 1)

        def p2_pool_h(eng, t, slot):
            eng.wait_ge(t_h2h, t + 1)
            plain(eng.tensor_tensor(h2[slot][1][:], hf[:], h2[slot][0][:].bitcast(F32), ALU.subtract)).then_inc(t_h2, 1)

        def p2_dve_gate(eng, t):
            base = GATE * t
            cnt = [0]

            def do(ins):
                cnt[0] += 1
                ins.then_inc(t_gate, 1)
                eng.wait_ge(t_gate, base + cnt[0])
            eng.wait_ge(t_GT, t + 1)
            do(eng.tensor_copy(logit[:], bank[3][:, 0:E]))
            do(plain(eng.max(top8[:], logit[:])))
            do(plain(eng.max_index(idx8[:], top8[:], logit[:])))
            do(eng.tensor_tensor(gv[:, 0:1], top8[:, 1:2], top8[:, 0:1], ALU.subtract))
            do(eng.tensor_copy(idxf[:], idx8[:]))
            eng.wait_ge(t_e, t + 1)
            do(eng.tensor_scalar(gv[:, 2:3], gv[:, 1:2], 1.0, None, ALU.add))
            do(eng.reciprocal(gv[:, 3:4], gv[:, 2:3]))
            do(eng.tensor_tensor(gv[:, 4:5], gv[:, 3:4], gv[:, 1:2], ALU.mult))
            eng.tensor_scalar(oneh[:, 0, :], iota_t[:], idxf[:, 0:1], gv[:, 3:4], ALU.is_equal, ALU.mult)
            do(eng.tensor_scalar(oneh[:, 1, :], iota_t[:], idxf[:, 1:2], gv[:, 4:5], ALU.is_equal, ALU.mult))
            assert cnt[0] == GATE
            eng.tensor_tensor(wfull[:], oneh[:, 0, :], oneh[:, 1, :], ALU.add).then_inc(t_wf, 1)
            eng.wait_ge(t_wf, t + 1)
            eng.wait_ge(t_U, t + 1)
            eng.wait_ge(t_UT, t + 1)
            eng.tensor_tensor(us[:], bank[2 + 0][:].rearrange("p (e r) -> p e r", r=R), wfull[:, :].unsqueeze(2).broadcast_to([P, E, R]),
                              ALU.mult).then_inc(t_us, 1)

        t_wf = sem("t_wf")

        def p2_dve_u(eng, t):
            eng.wait_ge(t_uh, t + 1)
            eng.tensor_tensor(usT[1][:], bank[5][:].rearrange("p (c q) -> p c q", q=P), usT[0][:].bitcast(F32), ALU.subtract).then_inc(t_ul, 1)

        def p2_dve_y(eng, t, slot, ld):
            eng.wait_ge(t_gb[slot], 16 * ld)
            gbs = tile_slot(gb, t)
            for half in range(2):
                cs = slice(half * 512, (half + 1) * 512)
                eng.wait_ge(t_Y, 2 * t + half + 1)
                if half == 0:
                    eng.wait_ge(t_out, 16 * t + 16)
                eng.tensor_tensor(yo[:, cs], bank[half][:], gbs[:, cs], ALU.mult).then_inc(t_y, 1)

        def p2_pool_y(eng, t, slot, ld):
            eng.wait_ge(t_x1[slot], 16 * ld)
            x1s = tile_slot(x1, t)
            for half in range(2):
                cs = slice(half * 512, (half + 1) * 512)
                eng.wait_ge(t_y, 2 * t + half + 3)
                plain(eng.tensor_tensor(yo[:, cs], yo[:, cs], x1s[:, cs], ALU.add)).then_inc(t_ya, 1)

        def p2_pool(eng):
            p2_pool_h(eng, 0, 0)
            p2_pool_h(eng, 1, 1)

            def body(t, slot, ld):
                p2_pool_h(eng, t + 1, 1 - slot)
                p2_pool_y(eng, t - 1, 1 - slot, ld if slot == 1 else ld - 1)
            tile_pairs(eng, body)
            p2_pool_y(eng, TILES - 2, 0, TILES // 2)
            p2_pool_y(eng, TILES - 1, 1, TILES // 2)

        def p2_dve(eng):
            for n, (src, dst, w) in enumerate(turned_weights()):
                eng.wait_ge(t_hi, n + 1)
                eng.tensor_tensor(dst[1], bank[n % 2][:, 0:w * len(src)], dst[0].bitcast(F32), ALU.subtract).then_inc(t_lo, 1)
            eng.wait_ge(t_in, T_IN)
            p2_dve_ln(eng, 0, 0, 1)
            p2_dve_ln(eng, 1, 1, 1)
            p2_dve_gate(eng, 0)
            p2_dve_u(eng, 0)

            def body(t, slot, ld):
                p2_dve_ln(eng, t + 1, 1 - slot, ld + (1 if slot == 1 else 0))
                p2_dve_gate(eng, t)
                p2_dve_y(eng, t - 1, 1 - slot, ld if slot == 1 else ld - 1)
                p2_dve_u(eng, t)
            tile_pairs(eng, body)
            t = TILES - 1
            p2_dve_gate(eng, t)
            p2_dve_y(eng, t - 1, 0, TILES // 2)
            p2_dve_u(eng, t)
            p2_dve_y(eng, t, 1, TILES // 2)

        def p2_pe(eng):
            eng.wait_ge(t_in, T_IN)
            for n, (src, dst, w) in enumerate(turned_weights()):
                if n >= 2:
                    eng.wait_ge(t_lo, n - 1)
                for j, s in enumerate(src):
                    k = s.shape[0]
                    m = eng.transpose(bank[n % 2][:, j * w:(j + 1) * w], s, ident_t[0:k, 0:k])
                m.then_inc(t_T, 1)

            def turn(t):
                eng.wait_ge(t_xn, t + 1)
                if not (isinstance(t, int) and t == 0):
                    eng.wait_ge(t_aff, 2 * t)
                for half in range(2):
                    for k in range(4 * half, 4 * half + 4):
                        m = eng.transpose(bank[6 + half][:, (k % 4) * P:(k % 4 + 1) * P], xn2[:, k * P:(k + 1) * P], ident_t[:])
                    m.then_inc(t_hT, 1)

            def up(t, slot):
                if isinstance(t, int) and t == 0:
                    eng.wait_ge(t_lo, NTURN)
                eng.wait_ge(t_h2, t + 2)
                eng.wait_ge(t_us, t + 1)
                for k in range(KT):
                    m = mm3(eng, bank[4][0:E, 0:P], sl(gT, lambda g: g[:, k, :]), sl(h2[slot], lambda h: h[:, k, :]), k == 0, k == KT - 1)
                m.then_inc(t_G, 1)
                for k in range(KT):
                    if k == KT // 2:
                        eng.wait_ge(t_lg, t + 1)
                        plain(eng.transpose(bank[3][:, 0:E], lgT[:], ident_t[0:E, 0:E])).then_inc(t_GT, 1)
                    m = mm3(eng, bank[2][:], sl(h2[slot], lambda h: h[:, k, :]), sl(aT, lambda a: a[:, k, :]), k == 0, k == KT - 1)
                m.then_inc(t_U, 1)

            def turn_u(t):
                eng.wait_ge(t_us, t + 2)
                eng.wait_ge(t_ul, t + 1)
                for cc in range(ET):
                    m = eng.transpose(bank[5][:, cc * P:(cc + 1) * P], us[:, 2 * cc:2 * cc + 2, :].rearrange("p e r -> p (e r)"), ident_t[:])
                m.then_inc(t_UT, 1)

            def down(t):
                eng.wait_ge(t_ul, t + 2)
                for half in range(2):
                    eng.wait_ge(t_y, 2 * t + half + 1)
                    for cc in range(ET):
                        m = mm3(eng, bank[half][:], sl(usT, lambda u: u[:, cc, :]), sl(bT, lambda w: w[:, cc, half * 512:(half + 1) * 512]),
                                cc == 0, cc == ET - 1)
                    m.then_inc(t_Y, 1)

            turn(0)
            up(0, 0)
            turn(1)
            turn_u(0)

            def body(t, slot, ld):
                up(t, slot)
                turn(t + 1)
                down(t - 1)
                turn_u(t)
            tile_pairs(eng, body)
            up(TILES - 1, 1)
            down(TILES - 2)
            turn_u(TILES - 1)
            down(TILES - 1)

        block = top.enter_context(nc.Block())

        @block.sync
        def _(eng):
            p0_sp(eng)
            p1_sp(eng)
            for i, s in enumerate(s_stage):
                eng.wait_ge(s, 16 * (5 * GROUPS + 1 - i))
            p2_sp(eng)
            attention_end(eng)
            p2_sp_tiles(eng)

        @block.gpsimd
        def _(eng):
            eng.sem_inc(s_split, 1)
            p1_pool(eng); attention_end(eng)
            p2_pool(eng)

        @block.scalar
        def _(eng):
            eng.sem_inc(s_x1, 16)
            act_load_x(eng, 0, range(QT))
            p0_act(eng)
            p1_act(eng); attention_end(eng)
            p2_act(eng)

        @block.vector
        def _(eng):
            eng.sem_inc(s_v, 1)
            eng.sem_inc(s_wor, 1)
            p0_dve(eng)
            p1_dve(eng); attention_end(eng)
            for s, credit in ((t_h2, 1), (t_us, 1), (t_ul, 1), (t_UT, 1), (t_y, 2)):
                eng.sem_inc(s, credit)
            p2_dve(eng)

        @block.tensor
        def _(eng):
            eng.sem_inc(s_proj, 1)
            eng.sem_inc(s_wo, 1)
            p0_pe(eng)
            p1_pe(eng); attention_end(eng)
            p2_pe(eng)


_INS = {"L0_attn_x": "x", "L0_attn_wq": "wq", "L0_attn_wk": "wk", "L0_attn_wv": "wv", "L0_attn_wo": "wo",
        "L0_ffn_gate_w": "gate_w", "L0_ffn_lora_A": "lora_a", "L0_ffn_lora_B": "lora_b", "L0_c": "c", "L0_wmod": "wmod"}


def kernel(**inputs):
    from concourse import bacc
    from concourse.bass_utils import run_bass_kernel_spmd

    nc = bacc.Bacc("TRN2", target_bir_lowering=False, num_devices=1)
    arrays, args = {}, {}
    given = {_INS[k]: np.ascontiguousarray(v) for k, v in inputs.items()} | constants()
    for name, a in given.items():
        arrays[f"in_{name}"] = a
        args[name] = nc.dram_tensor(f"in_{name}", a.shape, mybir.dt.from_np(a.dtype), kind="ExternalInput").ap()
    args["out"] = nc.dram_tensor("out", (BATCH, SEQ, D), F32, kind="ExternalOutput").ap()
    adaln_block(nc, **args)
    r = run_bass_kernel_spmd(nc, [arrays], core_ids=[0])
    return r.results[0]["out"]
```
